# Optimizing a Trainium2 kernel written in Bass

```python
import numpy as np
import jax
import jax.numpy as jnp

def _softmax(x, axis=-1):
    return jax.nn.softmax(x, axis=axis)

def _gelu(x):
    return jax.nn.gelu(x, approximate=True)

def _silu(x):
    return jax.nn.silu(x)

def _sigmoid(x):
    return jax.nn.sigmoid(x)

def _layernorm(x, axis=-1, eps=1e-05):
    m = jnp.mean(x, axis=axis, keepdims=True)
    v = jnp.var(x, axis=axis, keepdims=True)
    return (x - m) / jnp.sqrt(v + eps)

def _scatter_add(tgt, idx, src, axis=0):
    return tgt.at[idx].add(src)

def _segment_sum(src, seg, n):
    return jax.ops.segment_sum(src, seg, n)
kernel_name = 'mk_hybrid_d1_jaxref_r4_1f7057'

def setup_inputs(seed: int=0):
    np.random.seed(seed)
    _w = jnp.asarray

    def _L0_attn_a_setup():
        import jax, jax.numpy as jnp
        import numpy as np
        D_MODEL = 256
        N_HEADS = 16
        HEAD_DIM = D_MODEL // N_HEADS
        key = jax.random.key(seed)
        ks = jax.random.split(key, 9)
        s = 0.02
        x = jax.random.normal(ks[0], (2, 512, D_MODEL), dtype=jnp.float32)
        Wq = jax.random.normal(ks[1], (D_MODEL, D_MODEL), dtype=jnp.float32) * s
        bq = jnp.zeros((D_MODEL,), jnp.float32)
        Wk = jax.random.normal(ks[2], (D_MODEL, D_MODEL), dtype=jnp.float32) * s
        bk = jnp.zeros((D_MODEL,), jnp.float32)
        Wv = jax.random.normal(ks[3], (D_MODEL, D_MODEL), dtype=jnp.float32) * s
        bv = jnp.zeros((D_MODEL,), jnp.float32)
        Wo = jax.random.normal(ks[4], (D_MODEL, D_MODEL), dtype=jnp.float32) * s
        bo = jnp.zeros((D_MODEL,), jnp.float32)
        return {'x': x, 'Wq': Wq, 'bq': bq, 'Wk': Wk, 'bk': bk, 'Wv': Wv, 'bv': bv, 'Wo': Wo, 'bo': bo}
    _L0_attn_a_in = _L0_attn_a_setup()

    def _L0_attn_b_setup():
        import jax, jax.numpy as jnp
        import numpy as np
        B, L, D = (2, 512, 256)
        H = 16
        DH = D // H

        def rope_tables(seq_len, dim):
            inv_freq = 1.0 / 10000.0 ** (jnp.arange(0, dim, 2, dtype=jnp.float32) / dim)
            t = jnp.arange(seq_len, dtype=jnp.float32)
            freqs = jnp.outer(t, inv_freq)
            emb = jnp.concatenate([freqs, freqs], -1)
            return (jnp.cos(emb), jnp.sin(emb))

        def rotate_half(x):
            x1, x2 = (x[..., :x.shape[-1] // 2], x[..., x.shape[-1] // 2:])
            return jnp.concatenate([-x2, x1], axis=-1)
        key = jax.random.key(seed)
        k1, k2, k3 = jax.random.split(key, 3)
        x = jax.random.normal(k1, (B, L, D), dtype=jnp.float32)
        Wqkv = jax.random.normal(k2, (D, 3 * D), dtype=jnp.float32) / np.sqrt(D)
        Wo = jax.random.normal(k3, (D, D), dtype=jnp.float32) / np.sqrt(D)
        return {'x': x, 'Wqkv': Wqkv, 'Wo': Wo}
    _L0_attn_b_in = _L0_attn_b_setup()

    def _L0_ffn_setup():
        import jax, jax.numpy as jnp
        import numpy as np
        B, N, C, H, REG = (1, 2309, 256, 16, 5)
        D = C // H
        key = jax.random.key(seed)
        k0, k1, k2, k3 = jax.random.split(key, 4)
        x = jax.random.normal(k0, (B, N, C), dtype=jnp.float32)
        g_info = jax.random.normal(k1, (12, 2, C), dtype=jnp.float32)
        W_qkv = jax.random.normal(k2, (C, 3 * C), dtype=jnp.float32) * 0.02
        W_proj = jax.random.normal(k3, (C, C), dtype=jnp.float32) * 0.02
        b_proj = jnp.zeros((C,), dtype=jnp.float32)
        return {'x': x, 'g_info': g_info, 'W_qkv': W_qkv, 'W_proj': W_proj, 'b_proj': b_proj}
    _L0_ffn_in = _L0_ffn_setup()
    _d = {'L0_attn_a_x': _L0_attn_a_in['x'], 'L0_attn_a_Wq': _L0_attn_a_in['Wq'], 'L0_attn_a_bq': _L0_attn_a_in['bq'], 'L0_attn_a_Wk': _L0_attn_a_in['Wk'], 'L0_attn_a_bk': _L0_attn_a_in['bk'], 'L0_attn_a_Wv': _L0_attn_a_in['Wv'], 'L0_attn_a_bv': _L0_attn_a_in['bv'], 'L0_attn_a_Wo': _L0_attn_a_in['Wo'], 'L0_attn_a_bo': _L0_attn_a_in['bo'], 'L0_attn_b_Wqkv': _L0_attn_b_in['Wqkv'], 'L0_attn_b_Wo': _L0_attn_b_in['Wo'], 'L0_ffn_g_info': _L0_ffn_in['g_info'], 'L0_ffn_W_qkv': _L0_ffn_in['W_qkv'], 'L0_ffn_W_proj': _L0_ffn_in['W_proj'], 'L0_ffn_b_proj': _L0_ffn_in['b_proj']}
    _x0 = _d['L0_attn_a_x']
    _d['L0_attn_a_x'] = jax.random.normal(jax.random.fold_in(jax.random.key(seed), 1), (16, 512, 256), dtype=_x0.dtype)
    del _x0
    return _d

def reference(L0_attn_a_x, L0_attn_a_Wq, L0_attn_a_bq, L0_attn_a_Wk, L0_attn_a_bk, L0_attn_a_Wv, L0_attn_a_bv, L0_attn_a_Wo, L0_attn_a_bo, L0_attn_b_Wqkv, L0_attn_b_Wo, L0_ffn_g_info, L0_ffn_W_qkv, L0_ffn_W_proj, L0_ffn_b_proj):

    def _L0_attn_a_ref(x, Wq, bq, Wk, bk, Wv, bv, Wo, bo):
        import jax, jax.numpy as jnp
        import numpy as np
        D_MODEL = 256
        N_HEADS = 16
        HEAD_DIM = D_MODEL // N_HEADS
        b, seq, _ = x.shape
        Q = x @ Wq.T + bq
        K = x @ Wk.T + bk
        V = x @ Wv.T + bv

        def heads(t):
            return t.reshape(b, seq, N_HEADS, HEAD_DIM).transpose(0, 2, 1, 3)
        Qh, Kh, Vh = (heads(Q), heads(K), heads(V))
        scores = jnp.einsum('bhqd,bhkd->bhqk', Qh, Kh) / jnp.sqrt(jnp.float32(HEAD_DIM))
        idxs = jnp.arange(seq)
        mask = idxs[None, :] <= idxs[:, None]
        scores = jnp.where(mask[None, None], scores, jnp.float32(-10000.0))
        attn = jax.nn.softmax(scores, axis=-1)
        out_heads = jnp.einsum('bhqk,bhkd->bhqd', attn, Vh)
        out = out_heads.transpose(0, 2, 1, 3).reshape(b, seq, D_MODEL)
        return out @ Wo.T + bo

    def _L0_attn_b_ref(x, Wqkv, Wo):
        import jax, jax.numpy as jnp
        import numpy as np
        B, L, D = (2, 512, 256)
        H = 16
        DH = D // H

        def rope_tables(seq_len, dim):
            inv_freq = 1.0 / 10000.0 ** (jnp.arange(0, dim, 2, dtype=jnp.float32) / dim)
            t = jnp.arange(seq_len, dtype=jnp.float32)
            freqs = jnp.outer(t, inv_freq)
            emb = jnp.concatenate([freqs, freqs], -1)
            return (jnp.cos(emb), jnp.sin(emb))

        def rotate_half(x):
            x1, x2 = (x[..., :x.shape[-1] // 2], x[..., x.shape[-1] // 2:])
            return jnp.concatenate([-x2, x1], axis=-1)
        b, l, d = x.shape
        qkv = (x @ Wqkv).reshape(b, l, 3, H, DH)
        q, k, v = (qkv[:, :, 0], qkv[:, :, 1], qkv[:, :, 2])
        cos, sin = rope_tables(l, DH)
        cos = cos[:, None, :]
        sin = sin[:, None, :]
        q = q * cos + rotate_half(q) * sin
        k = k * cos + rotate_half(k) * sin
        scale = DH ** (-0.5)
        scores = jnp.einsum('bqhd,bkhd->bhqk', q, k) * scale
        attn = jax.nn.softmax(scores, axis=-1)
        out = jnp.einsum('bhqk,bkhd->bqhd', attn, v)
        out = out.reshape(b, l, d)
        return out @ Wo

    def _L0_ffn_ref(x, g_info, W_qkv, W_proj, b_proj):
        import jax, jax.numpy as jnp
        import numpy as np
        B, N, C, H, REG = (1, 2309, 256, 16, 5)
        D = C // H
        Bx, Nx, Cx = x.shape
        scale = D ** (-0.5)
        qkv = (x @ W_qkv).reshape(Bx, Nx, 3, H, D)
        q, k, v = (qkv[:, :, 0], qkv[:, :, 1], qkv[:, :, 2])
        g_layer = g_info[0].reshape(-1, H, D)
        q_g = g_layer[0]
        q_pure = q[:, REG:]
        q_n = q_pure / jnp.linalg.norm(q_pure, axis=-1, keepdims=True)
        qg_n = q_g / jnp.linalg.norm(q_g, axis=-1, keepdims=True)
        sim = (qg_n[None, None] * q_n).sum(-1).mean(-1)
        sim = (sim - sim.min()) / (sim.max() - sim.min())
        pos = sim > 0.9
        logits = jnp.einsum('bqhd,bkhd->bhqk', q * scale, k)

        def masked_attn(tok_mask):
            key_mask = jnp.concatenate([jnp.ones((Bx, REG), bool), tok_mask], axis=1)
            l = jnp.where(key_mask[:, None, None, :], logits, -jnp.inf)
            a = jax.nn.softmax(l, axis=-1)
            return jnp.einsum('bhqk,bkhd->bqhd', a, v)
        x_pos = masked_attn(pos)
        x_neg = masked_attn(~pos)
        reg_out = (x_pos[:, :REG] + x_neg[:, :REG]) * 0.5
        tok_out = jnp.where(pos[:, :, None, None], x_pos[:, REG:], x_neg[:, REG:])
        out = jnp.concatenate([reg_out, tok_out], axis=1).reshape(Bx, Nx, Cx)
        return out @ W_proj + b_proj
    x = L0_attn_a_x
    x = x + _L0_attn_a_ref(_layernorm(x, axis=-1), L0_attn_a_Wq, L0_attn_a_bq, L0_attn_a_Wk, L0_attn_a_bk, L0_attn_a_Wv, L0_attn_a_bv, L0_attn_a_Wo, L0_attn_a_bo)
    x = x + _L0_ffn_ref(_layernorm(x, axis=-1), L0_ffn_g_info, L0_ffn_W_qkv, L0_ffn_W_proj, L0_ffn_b_proj)
    x = x + _L0_attn_b_ref(_layernorm(x, axis=-1), L0_attn_b_Wqkv, L0_attn_b_Wo)
    x = x + _L0_ffn_ref(_layernorm(x, axis=-1), L0_ffn_g_info, L0_ffn_W_qkv, L0_ffn_W_proj, L0_ffn_b_proj)
    return x

_drawn_inputs = setup_inputs


def setup_inputs(seed=0):
    import zlib

    import numpy as np

    out = dict(_drawn_inputs(seed))
    spreads = {'L0_attn_a_bq': (0.0, 0.8),
     'L0_attn_a_bk': (0.0, 0.8),
     'L0_attn_a_bv': (0.0, 0.1),
     'L0_attn_a_bo': (0.0, 0.1),
     'L0_ffn_b_proj': (0.0, 0.1)}
    factors = {'L0_attn_a_Wq': 8.0, 'L0_attn_a_Wk': 8.0, 'L0_attn_a_Wv': 4.213, 'L0_ffn_g_info': 8.0}
    for name, (base, spread) in spreads.items():
        noise = np.random.default_rng([zlib.crc32(name.encode()), seed]).standard_normal(out[name].shape)
        drawn = base * np.exp(spread * noise) if base else spread * noise
        out[name] = jnp.asarray(drawn.astype(out[name].dtype))
    for name, factor in factors.items():
        out[name] = (out[name] * factor).astype(out[name].dtype)
    return out
```

```python
from contextlib import ExitStack

import concourse.bass as bass
from concourse import mybir

F32 = mybir.dt.float32
BF16 = mybir.dt.bfloat16
ALU = mybir.AluOpType
ACT = mybir.ActivationFunctionType
AX = mybir.AxisListType

P = 128
NB = 16
L = 512
D = 256
H = 16
DH = D // H
T = L // P
KT = D // P
G = 4
NG = H // G
REG = 5
XW = 32
EPS = 1e-5
PARTS = 6 * DH
MASK = PARTS
SHIFT = PARTS + 2
ROWS = PARTS + 4
VW = DH + 1
AHEAD = 6
BIG = float(2.0 ** 100)

CAUSAL, SPLIT, ROTARY = "causal", "split", "rotary"
STAGES = [CAUSAL, SPLIT, ROTARY, SPLIT]

Q_BLOCKS = [0, 0, 0, 1, 1, 2]
K_BLOCKS = [0, 1, 2, 0, 1, 0]

TURNS = {
    1: [("xt", 1, 0), ("xt", 1, 1)],
    2: [("sh", 0, 1), ("ex", 0, 0), ("qk", 1, 0)],
    3: [("qk", 1, 1)],
    4: [("qk", 1, 2), ("qk", 1, 3)],
    5: [("v", 1, 0)],
    6: [("sh", 0, 2), ("ex", 0, 1)],
    7: [("v", 1, 1)],
    8: [("ot", -1, 0)],
    9: [("ot", -1, 1)],
    10: [("sh", 0, 3), ("ex", 0, 2)],
    11: [("out", -1, 0)],
    12: [("out", -1, 1)],
    14: [("sh", 1, 0), ("ex", 0, 3)],
}
PREPARE = [("xt", 0), ("xt", 1), ("qk", 0), ("qk", 1), ("qk", 2), ("qk", 3), ("v", 0), ("v", 1)]
FINISH = [("ot", 0), ("ot", 1), ("out", 0), ("out", 1)]


def turns_of(kind, b, slot):
    return [t for t in TURNS.get(slot, []) if b + t[1] < NB and (t[0] != "ex" or kind == SPLIT)]


def max_head(b, slot):
    h = slot + AHEAD
    off, h = (0, h) if h < H else (1, h - H)
    return (off, h) if b + off < NB else None


def key_start(kind, kt):
    return kt * P if kind == CAUSAL else 0


def prob_offset(kind, kt):
    return [0, 512, 1024, 1280][kt] if kind == CAUSAL else kt * L


class Batch:

    def __init__(self, s, n, turn=None):
        self.s, self.n, self.turn = s, n, turn

    def __add__(self, k):
        return Batch(self.s, self.n + k, self.turn)

    def index(self):
        return self.n if self.turn is None else self.turn * 2 + self.n

    def one(self):
        return bass.ds(self.index(), 1)


LOOPS = (NB - 2) // 2


def over_batches(eng, body):
    body(0)
    with eng.Fori(1, NB, 1) as b:
        body(b)


def wait_before(eng, sem, b, base, still=None):
    if not isinstance(b, int) or b + base:
        wait_reg(eng, sem, b + base, still)


def wait_reg(eng, sem, value, still=None):
    eng.wait_ge(sem, value)
    if still is not None and not isinstance(value, int):
        eng.sem_inc(still, 1)


class Count:

    def __init__(self, sem, labels, step=1):
        self.sem, self.step = sem, step
        self.at = {lab: (i + 1) * step for i, lab in enumerate(labels)}
        assert len(self.at) == len(labels)

    def after(self, B, *label):
        lab = lambda n: (B.s, n) + label
        if B.turn is None:
            return self.at[lab(B.n)]
        second = self.at[lab(B.n + 2)]
        d = self.at[lab(B.n + 4)] - second
        c = second - d
        assert c > 0 and all(self.at.get(lab(B.n + 2 * i), c) == c + d * i for i in range(LOOPS))
        return B.turn * d + c

    def wait(self, eng, B, *label, still=None):
        if B.turn is None and B.n < 0:
            return
        wait_reg(eng, self.sem, self.after(B, *label), still)

    def wait_earlier(self, eng, B, back, *label):
        v = self.after(B, *label) - self.step * back
        if B.turn is None and v <= 0:
            return
        eng.wait_ge(self.sem, v)

    def position(self, B, *label):
        return self.at[(B.s, B.n) + label] // self.step - 1


def steps_of(per_body, first=None, last=None):
    out = []
    for s, kind in enumerate(STAGES):
        if first:
            out += [(s, 0) + lab for lab in first(kind)]
        for b in range(NB):
            out += [(s, b + off) + lab for off, lab in per_body(kind, b)]
        if last:
            out += [(s, NB - 1) + lab for lab in last(kind)]
    return out


def hybrid_blocks(nc, x_in, w, consts, out):
    ctx = ExitStack()
    with ctx:
        def sb(name, shape, dt=F32):
            return ctx.enter_context(nc.sbuf_tensor(name, shape, dt))

        def ps(name, shape):
            return ctx.enter_context(nc.psum_tensor(name, shape, F32))

        def sem(name):
            return ctx.enter_context(nc.semaphore(name))

        xs = [x_in] + [nc.dram_tensor(f"x_after_{s}", (NB, L, D), F32, kind="Internal").ap() for s in range(3)] + [out]
        q_stack_d = nc.dram_tensor("q_stack_d", (NB, SHIFT, H, L), BF16, kind="Internal").ap()
        k_stack_d = nc.dram_tensor("k_stack_d", (NB, SHIFT, H, L), BF16, kind="Internal").ap()
        mask_d = nc.dram_tensor("mask_d", (4, NB * L), BF16, kind="Internal").ap()

        wq = {k: sb(f"wq_{k}", [P, KT, D]) for k in (CAUSAL, SPLIT, ROTARY)}
        wk = {k: sb(f"wk_{k}", [P, KT, D]) for k in (CAUSAL, SPLIT, ROTARY)}
        wv = {k: sb(f"wv_{k}", [P, KT, D]) for k in (CAUSAL, SPLIT, ROTARY)}
        wo = {k: sb(f"wo_{k}", [P, KT, D]) for k in (CAUSAL, SPLIT, ROTARY)}
        wq_class = sb("wq_class", [P, KT, D])
        qk_bias = sb("qk_bias", [P, 2 * KT])
        q_bias = sb("q_bias", [P, KT])
        v_bias = sb("v_bias", [P, D])
        o_bias = {CAUSAL: sb("o_bias_c", [P, D]), SPLIT: sb("o_bias_s", [P, D])}
        cos_t = sb("cos_t", [P, L])
        sin_t = sb("sin_t", [P, L])
        ident = sb("ident", [P, P])
        ident_b = sb("ident_b", [P, P], BF16)
        causal_kq = sb("causal_kq", [P, P], BF16)
        causal_qk = sb("causal_qk", [P, P], BF16)
        guide = sb("guide", [P, D])
        minus_half = sb("minus_half", [P, T * H])
        reg_big = sb("reg_big", [P, NB * T])

        x_new = sb("x_new", [P, 2, T, D])
        bn = sb("bn", [P, T, 6])
        mean_var = sb("mean_var", [P, T, 2])
        var_eps = sb("var_eps", [P, T])
        rstd = sb("rstd", [P, T])
        xn = sb("xn", [P, T, D])
        xn_t = sb("xn_t", [P, KT, L])
        qk_f = sb("qk_f", [P, 4, L])
        rot_a = sb("rot_a", [P, L])
        rot_b = sb("rot_b", [P, L])
        rot_f = sb("rot_f", [P, KT, L])
        rest = sb("rest", [P, L])
        parts = sb("parts", [P, 4, 3, L], BF16)
        q_stack = [sb(f"q_stack{i}", [P, H, L], BF16) for i in range(2)]
        k_stack = [sb(f"k_stack{i}", [P, H, L], BF16) for i in range(2)]
        qx = [sb(f"qx{i}", [P, H, XW], BF16) for i in range(2)]
        values = [sb(f"values{i}", [P, T, H, VW]) for i in range(2)]
        neg_max = sb("neg_max", [P, G, T])
        shift_parts = sb("shift_parts", [P, 2, G * T], BF16)
        shift_rows = sb("shift_rows", [2 * G * T, P], BF16)
        probs = [sb(f"probs{i}", [P, T * L]) for i in range(2)]
        x_neg_max = sb("x_neg_max", [P, 1])
        x_probs = sb("x_probs", [P, L])
        x_probs_t = sb("x_probs_t", [P, T, P])
        inv_sum = sb("inv_sum", [P, G, T])
        x_inv = sb("x_inv", [P, G])
        x_half = sb("x_half", [P, G])
        x_out = sb("x_out", [P, G, DH])
        att = [sb(f"att{i}", [P, T, D]) for i in range(2)]
        att_t = sb("att_t", [P, KT, L])
        x_res = sb("x_res", [P, T, D])

        prod = probs[0][:, 0:T * D].rearrange("p (t d) -> p t d", t=T)
        square = probs[1][:, 0:T * D].rearrange("p (t d) -> p t d", t=T)
        dots = sb("dots", [P, T * H])
        norms = sb("norms", [P, T * H])
        cosines = sb("cosines", [P, T * H])
        sim_b = sb("sim_b", [P, T])
        sim = sb("sim", [P, NB * T])
        extremes = sb("extremes", [P, 2])
        all_extremes = sb("all_extremes", [P, 2])
        spread = sb("spread", [P, 2])
        cls = sb("cls", [P, 3, NB * T])
        class_rows = sb("class_rows", [P, 4, NB * T], BF16)
        class_t = sb("class_t", [P, 2, P], BF16)

        st = [ps(f"scores_t{i}", [P, 2 * L]) for i in range(2)]
        sm = [ps(f"scores{i}", [P, L]) for i in range(2)]
        o_ps = ps("o_ps", [P, L])
        turn_ps = ps("turn_ps", [P, L])
        o_main = o_ps[:, 0:G * T * VW].rearrange("p (h t c) -> p h t c", h=G, t=T)
        o_extra = o_ps[:, G * T * VW:G * T * VW + G * VW].rearrange("p (h c) -> p h c", h=G)
        turn_b = turn_ps[:, 0:P // 2].bitcast(BF16)
        turn_b2 = turn_ps[:, P // 2:P].bitcast(BF16)

        def turn_steps(kind, b):
            return [(off, (k, i)) for slot in range(H) for k, off, i in turns_of(kind, b, slot)]

        turn_args = (turn_steps, lambda kind: PREPARE + [("sh", 0)], lambda kind: FINISH)
        turn_full = Count(sem("turn_full"), steps_of(*turn_args))
        turn_free = Count(sem("turn_free"), steps_of(*turn_args))

        def max_steps(kind, b):
            res = []
            for slot in range(H):
                m = max_head(b, slot)
                if m:
                    res += [(m[0], (m[1], t)) for t in range(T)]
                if kind == SPLIT and slot % G == 1:
                    res.append((0, ("extra", slot // G)))
            return res

        max_args = (max_steps, lambda kind: [(h, t) for h in range(AHEAD) for t in range(T)])
        sm_full = Count(sem("scores_full"), steps_of(*max_args))
        max_done = Count(sem("max_done"), steps_of(*max_args))

        chunks = (lambda kind, b: [(0, (h, c)) for h in range(H) for c in range(2)],)
        heads = (lambda kind, b: [(0, (h,)) for h in range(H)],)
        groups = (lambda kind, b: [(0, (g,)) for g in range(NG)],)
        st_full = Count(sem("scores_t_full"), steps_of(*chunks))
        exp_done = Count(sem("exp_done"), steps_of(*chunks))
        pv_done = Count(sem("pv_done"), steps_of(*heads))
        o_read = Count(sem("o_read"), steps_of(*groups))
        o_inv = Count(sem("o_inv"), steps_of(*groups))

        def per_group_shift(kind, b):
            return [(off, (i,)) for slot in range(H) for k, off, i in turns_of(kind, b, slot) if k == "sh"]

        shift_args = (per_group_shift, lambda kind: [(0,)])
        shift_high = Count(sem("shift_high"), steps_of(*shift_args))
        shift_ready = Count(sem("shift_ready"), steps_of(*shift_args))
        shift_in = Count(sem("shift_in"), steps_of(*shift_args), 16)

        nexts = (lambda kind, b: [(1, ())] if b + 1 < NB else [], lambda kind: [()])
        x_loaded = Count(sem("x_loaded"), steps_of(*nexts), 16)
        bn_done = Count(sem("bn_done"), steps_of(*nexts))
        stats_done = Count(sem("stats_done"), steps_of(*nexts))
        eps_done = Count(sem("eps_done"), steps_of(*nexts))
        rstd_done = Count(sem("rstd_done"), steps_of(*nexts))
        xn_done = Count(sem("xn_done"), steps_of(*nexts))
        qx_done = Count(sem("qx_done"), steps_of(*nexts))
        q_in = Count(sem("q_in"), steps_of(*nexts), 16)
        k_in = Count(sem("k_in"), steps_of(*nexts), 16)

        def of_next(items):
            return (lambda kind, b: [(1, i) for i in items] if b + 1 < NB else [], lambda kind: list(items))

        split_steps = Count(sem("split_steps"), steps_of(*of_next([(j, i) for j in range(4) for i in range(4)])))
        rot_steps = Count(sem("rot_steps"), steps_of(*of_next([(j, i) for j in range(4) for i in range(3)])))
        parts_out = Count(sem("parts_out"), steps_of(*of_next([(j, i) for j in range(4) for i in range(6)])), 16)

        prevs = (lambda kind, b: [(-1, ())] if b else [], None, lambda kind: [()])
        res_loaded = Count(sem("res_loaded"), steps_of(*prevs), 16)
        res_biased = Count(sem("res_biased"), steps_of(*prevs))
        res_halves = (lambda kind, b: [(-1, (v,)) for v in range(2)] if b else [], None, lambda kind: [(0,), (1,)])
        res_done = Count(sem("res_done"), steps_of(*res_halves))
        stored = Count(sem("stored"), steps_of(lambda kind, b: [(-1, ())], None, lambda kind: [()]), 16)

        xmax_exp = Count(sem("extra_exp"), steps_of(lambda kind, b: [(0, (g,)) for g in range(NG)] if kind == SPLIT else []))
        extra_steps = Count(sem("extra_steps"), steps_of(lambda kind, b: [(0, (g, i)) for g in range(NG) for i in range(4)]))

        consts_in = sem("consts_in")
        preset = sem("preset")
        masks_cleared = sem("masks_cleared")
        c_x = sem("c_x"); c_bn = sem("c_bn"); c_stats = sem("c_stats"); c_eps = sem("c_eps")
        c_rstd = sem("c_rstd"); c_xn = sem("c_xn"); c_tr = sem("c_tr"); c_trc = sem("c_trc")
        c_q = sem("c_q"); c_prod = sem("c_prod"); c_sq = sem("c_sq"); c_dots = sem("c_dots")
        c_norm = sem("c_norm"); c_inv = sem("c_inv"); c_cos = sem("c_cos"); c_simb = sem("c_simb")
        c_sim = sem("c_sim"); c_ext = sem("c_ext"); c_all = sem("c_all"); c_step = sem("c_step")
        c_rows = sem("c_rows"); c_rt = sem("c_rt"); c_rtc = sem("c_rtc"); c_dram = sem("c_dram")
        c_masks = sem("c_masks"); g_step = sem("g_step")

        still = sem("passed")

        block = ctx.enter_context(nc.Block())

        def run_stage(eng, s, first, body, finish):
            first(Batch(s, 0))
            body(Batch(s, 0))
            with eng.Fori(0, LOOPS, 1) as i:
                body(Batch(s, 1, i))
                body(Batch(s, 2, i))
            body(Batch(s, NB - 1))
            finish(Batch(s, NB - 1))

        def stage_start(eng, s):
            if s:
                eng.wait_ge(stored.sem, 16 * (NB + 1) * s)
            else:
                eng.wait_ge(consts_in, 16 * len(loads))
                eng.wait_ge(preset, PRESETS)

        nothing = lambda B: None

        loads = []
        for k in (CAUSAL, SPLIT, ROTARY):
            for tile, name in ((wq, "wq"), (wk, "wk"), (wv, "wv"), (wo, "wo")):
                loads.append((tile[k][:, :, :], w[f"{name}_{k}"].rearrange("(k p) n -> p k n", p=P)))
        loads.append((wq_class[:, :, :], w["wq_class"].rearrange("(k p) n -> p k n", p=P)))
        for tile, name in ((qk_bias, "qk_bias"), (v_bias, "v_bias"), (o_bias[CAUSAL], "o_bias_causal"),
                           (o_bias[SPLIT], "o_bias_split"), (guide, "guide")):
            loads.append((tile[:, :], w[name]))
        for tile, name in ((cos_t, "cos"), (sin_t, "sin"), (ident, "ident"), (ident_b, "ident_b"),
                           (causal_kq, "causal_kq"), (causal_qk, "causal_qk"), (reg_big, "reg_big")):
            loads.append((tile[:, :], consts[name]))
        for i in range(2):
            loads.append((qx[i][MASK:MASK + 2, :, :].rearrange("p h c -> p (h c)"), consts["neg_class"]))
        PRESETS = 4 * 2 + 1 + 2
        QX_ROWS = PARTS

        @block.sync
        def _(sp):
            for dst, src in loads:
                sp.dma_start(dst, src).then_inc(consts_in, 16)
            stage_start(sp, 0)

            def load_x(B):
                xn_done.wait(sp, B + (-2), still=still)
                sp.dma_start(x_new[:, B.n % 2, :, :],
                             xs[B.s][B.one()].rearrange("a (t p) d -> p (a t) d", p=P)).then_inc(x_loaded.sem, 16)

            def load_stack(B, q):
                kind = STAGES[B.s]
                tile, dram, blocks, here = ((q_stack, q_stack_d, Q_BLOCKS, q_in) if q
                                            else (k_stack, k_stack_d, K_BLOCKS, k_in))
                for j in ((0, 1) if q else (2, 3)):
                    split_steps.wait(sp, B, j, 3, still=still)
                    for i, part in enumerate(blocks):
                        row = DH * i + 8 * (j % 2)
                        sp.dma_start(dram[B.one(), row:row + 8].rearrange("a r h t -> (a r h) t"),
                                     parts[:, j, part, :]).then_inc(parts_out.sem, 16)
                parts_out.wait(sp, B, 1 if q else 3, 5, still=still)
                if B.n >= 2 or B.turn is not None:
                    st_full.wait(sp, B + (-2), H - 1, 1, still=still)
                    if q:
                        qx_done.wait(sp, B + (-2), still=still)
                rows = SHIFT if kind == SPLIT else PARTS
                sp.dma_start(tile[B.n % 2][0:rows, :, :],
                             dram[B.one(), 0:rows].rearrange("a r h t -> (a r) h t")).then_inc(here.sem, 16)

            def shift_dma(B, g):
                turn_free.wait(sp, B, "sh", g, still=still)
                sp.dma_start(q_stack[B.n % 2][SHIFT:SHIFT + 2, G * g:G * g + G, :],
                             shift_rows[:, :]).then_inc(shift_in.sem, 16)

            def load_residual(B):
                stored.wait(sp, B + (-1), still=still)
                sp.dma_start(x_res[:, :, :],
                             xs[B.s][B.one()].rearrange("a (t p) d -> p (a t) d", p=P)).then_inc(res_loaded.sem, 16)

            def store(B):
                res_done.wait(sp, B, 1, still=still)
                sp.dma_start(xs[B.s + 1][B.one()].rearrange("a (t p) d -> p (a t) d", p=P),
                             x_res[:, :, :]).then_inc(stored.sem, 16)

            def first(B):
                load_x(B)
                load_stack(B, True)
                load_stack(B, False)
                shift_dma(B, 0)

            def body(B):
                nxt = B.n + 1 < NB
                if nxt:
                    load_x(B + 1)
                if B.n:
                    load_residual(B + (-1))
                else:
                    sp.sem_inc(stored.sem, 16)
                shift_dma(B, 1)
                if nxt:
                    load_stack(B + 1, True)
                shift_dma(B, 2)
                if nxt:
                    load_stack(B + 1, False)
                shift_dma(B, 3)
                if B.n:
                    store(B + (-1))
                if nxt:
                    shift_dma(B + 1, 0)

            def finish(B):
                load_residual(B)
                store(B)

            n_class = 0
            for s, kind in enumerate(STAGES):
                if s:
                    stage_start(sp, s)
                if kind == SPLIT:
                    base = NB * n_class
                    def class_batch(b, base=base):
                        wait_before(sp, c_xn, b, base, still)
                        sp.dma_start(x_new[:, 0, :, :],
                                     xs[s][bass.ds(b, 1)].rearrange("a (t p) d -> p (a t) d", p=P)).then_inc(c_x, 16)

                    over_batches(sp, class_batch)
                    sp.wait_ge(c_rtc, n_class + 1)
                    sp.dma_start(mask_d.rearrange("k (b t) -> (k b) t", t=P).rearrange("(a c) t -> c a t", a=2),
                                 class_t[:, :, :]).then_inc(c_dram, 16)
                    sp.wait_ge(c_dram, 16 * (n_class + 1))
                    n = 0
                    for r in range(4):
                        dram = q_stack_d if r < 2 else k_stack_d
                        for h in range(H):
                            sp.dma_start(dram[:, MASK + r % 2, h, :],
                                         mask_d[r].rearrange("(b t) -> b t", b=NB)).then_inc(c_masks, 16)
                            n += 1
                    n_class += 1
                    sp.wait_ge(c_masks, 16 * n * n_class)
                run_stage(sp, s, first, body, finish)
            sp.wait_ge(stored.sem, 16 * (NB + 1) * len(STAGES))

        @block.gpsimd
        def _(pool):
            for i in range(2):
                nc.gpsimd.memset(values[i][:, :, :, DH:VW], 1.0).then_inc(preset, 1)
            nc.gpsimd.memset(minus_half[:, :], -0.5).then_inc(preset, 1)
            stage_start(pool, 0)

            def normalise(B):
                stats_done.wait(pool, B, still=still)
                nc.gpsimd.tensor_scalar(var_eps[:, :], mean_var[:, :, 1], EPS, None, ALU.add).then_inc(eps_done.sem, 1)
                eps_done.wait(pool, B, still=still)
                nc.gpsimd.tensor_tensor(rstd[:, :], var_eps[:, :], minus_half[:, 0:T], ALU.pow).then_inc(rstd_done.sem, 1)
                rstd_done.wait(pool, B, still=still)
                if B.n:
                    turn_full.wait(pool, B + (-1), "xt", 1, still=still)
                for t in range(T):
                    last = nc.gpsimd.tensor_scalar(xn[:, t, :], x_new[:, B.n % 2, t, :], mean_var[:, t, 0:1],
                                                   rstd[:, t:t + 1], ALU.subtract, ALU.mult)
                last.then_inc(xn_done.sem, 1)

            def rotate(B, q):
                a, b = (0, 1) if q else (2, 3)
                turn_free.wait(pool, B, "qk", b, still=still)
                if q:
                    if B.n:
                        split_steps.wait(pool, B + (-1), 3, 3, still=still)
                else:
                    split_steps.wait(pool, B, 1, 3, still=still)
                for j, (own, other, op) in enumerate(((a, b, ALU.subtract), (b, a, ALU.add))):
                    if j:
                        rot_steps.wait(pool, B, a, 2, still=still)
                    nc.gpsimd.tensor_tensor(rot_a[:, :], qk_f[:, own, :], cos_t[:, :], ALU.mult).then_inc(rot_steps.sem, 1)
                    nc.gpsimd.tensor_tensor(rot_b[:, :], qk_f[:, other, :], sin_t[:, :], ALU.mult).then_inc(rot_steps.sem, 1)
                    rot_steps.wait(pool, B, a + j, 1, still=still)
                    nc.gpsimd.tensor_tensor(rot_f[:, j, :], rot_a[:, :], rot_b[:, :], op).then_inc(rot_steps.sem, 1)

            def split(B, j, src):
                if B.n:
                    parts_out.wait(pool, B + (-1), j, 5, still=still)
                nc.gpsimd.tensor_copy(parts[:, j, 0, :], src).then_inc(split_steps.sem, 1)
                split_steps.wait(pool, B, j, 0, still=still)
                nc.gpsimd.tensor_tensor(rest[:, :], src, parts[:, j, 0, :], ALU.subtract).then_inc(split_steps.sem, 1)
                split_steps.wait(pool, B, j, 1, still=still)
                nc.gpsimd.tensor_copy(parts[:, j, 1, :], rest[:, :]).then_inc(split_steps.sem, 1)
                split_steps.wait(pool, B, j, 2, still=still)
                nc.gpsimd.tensor_tensor(parts[:, j, 2, :], rest[:, :], parts[:, j, 1, :], ALU.subtract).then_inc(split_steps.sem, 1)

            def splits(B, q):
                rotary = STAGES[B.s] == ROTARY
                if rotary:
                    rotate(B, q)
                for m in range(2):
                    j = m + (0 if q else 2)
                    if rotary:
                        rot_steps.wait(pool, B, j, 2, still=still)
                        split(B, j, rot_f[:, m, :])
                    else:
                        turn_free.wait(pool, B, "qk", j, still=still)
                        split(B, j, qk_f[:, j, :])
                        pool.sem_inc(rot_steps.sem, 3)

            def bias_residual(B):
                res_loaded.wait(pool, B, still=still)
                kind = STAGES[B.s]
                if kind == ROTARY:
                    pool.sem_inc(res_biased.sem, 1)
                else:
                    nc.gpsimd.tensor_tensor(x_res[:, :, :], x_res[:, :, :],
                                            o_bias[kind][:, :].unsqueeze(1).broadcast_to([P, T, D]),
                                            ALU.add).then_inc(res_biased.sem, 1)

            def first(B):
                normalise(B)
                splits(B, True)
                splits(B, False)

            def body(B):
                nxt = B.n + 1 < NB
                if nxt:
                    normalise(B + 1)
                if B.n:
                    bias_residual(B + (-1))
                if nxt:
                    splits(B + 1, True)
                    splits(B + 1, False)

            n_class = 0
            for s, kind in enumerate(STAGES):
                if s:
                    stage_start(pool, s)
                if kind == SPLIT:
                    base = NB * n_class
                    if n_class == 0:
                        pool.wait_ge(g_step, 2)
                        nc.gpsimd.tensor_tensor(norms[:, 0:H], norms[:, H:2 * H], minus_half[:, 0:H], ALU.pow).then_inc(g_step, 1)
                    def class_batch(b, base=base):
                        wait_reg(pool, c_stats, b + (base + 1), still)
                        nc.gpsimd.tensor_scalar(var_eps[:, :], mean_var[:, :, 1], EPS, None, ALU.add).then_inc(c_eps, 1)
                        wait_reg(pool, c_eps, b + (base + 1), still)
                        nc.gpsimd.tensor_tensor(rstd[:, :], var_eps[:, :], minus_half[:, 0:T], ALU.pow).then_inc(c_rstd, 1)
                        wait_reg(pool, c_rstd, b + (base + 1), still)
                        wait_before(pool, c_tr, b, base, still)
                        for t in range(T):
                            last = nc.gpsimd.tensor_scalar(xn[:, t, :], x_new[:, 0, t, :], mean_var[:, t, 0:1],
                                                           rstd[:, t:t + 1], ALU.subtract, ALU.mult)
                        last.then_inc(c_xn, 1)
                        wait_reg(pool, c_norm, b + (base + 1), still)
                        nc.gpsimd.tensor_tensor(cosines[:, :], norms[:, :], minus_half[:, :], ALU.pow).then_inc(c_inv, 1)

                    over_batches(pool, class_batch)
                    pool.wait_ge(c_ext, n_class + 1)
                    nc.gpsimd.partition_all_reduce(all_extremes[:, :], extremes[:, :], P, bass.bass_isa.ReduceOp.max).then_inc(c_all, 1)
                    n_class += 1
                run_stage(pool, s, first, body,
                          lambda B: bias_residual(B))

        @block.vector
        def _(dve):
            for i in range(2):
                nc.vector.memset(q_stack[i][PARTS:ROWS, :, :], 0.0).then_inc(preset, 1)
                nc.vector.memset(k_stack[i][PARTS:ROWS, :, :], 1.0).then_inc(preset, 1)
                nc.vector.memset(qx[i][0:QX_ROWS, :, :], 0.0).then_inc(preset, 1)
            nc.vector.memset(sm[0][:, :], 0.0).then_inc(preset, 1)
            nc.vector.memset(sm[1][:, :], 0.0).then_inc(preset, 1)
            stage_start(dve, 0)

            def statistics(B):
                x_loaded.wait(dve, B)
                for t in range(T):
                    last = nc.vector.bn_stats(bn[:, t, :], x_new[:, B.n % 2, t, :])
                last.then_inc(bn_done.sem, 1)
                if B.n:
                    xn_done.wait(dve, B + (-1))
                bn_done.wait(dve, B, still=still)
                for t in range(T):
                    last = nc.vector.bn_aggr(mean_var[:, t, :], bn[:, t, :])
                last.then_inc(stats_done.sem, 1)

            def register_queries(B):
                if STAGES[B.s] == SPLIT:
                    q_in.wait(dve, B)
                    if B.n >= 2 or B.turn is not None:
                        sm_full.wait(dve, B + (-2), "extra", NG - 1)
                    nc.vector.tensor_copy(qx[B.n % 2][0:PARTS, :, 0:8],
                                          q_stack[B.n % 2][0:PARTS, :, 0:8]).then_inc(qx_done.sem, 1)
                else:
                    dve.sem_inc(qx_done.sem, 1)

            def maxima(B, h):
                kind = STAGES[B.s]
                if h % G == 0 and (h or B.n):
                    shift_ready.wait(dve, B + (0 if h else -1), (h // G - 1) % NG)
                for t in range(T):
                    sm_full.wait(dve, B, h, t)
                    n = (t + 1) * P if kind == CAUSAL else L
                    bank = sm[sm_full.position(B, h, t) % 2]
                    nc.vector.tensor_reduce(neg_max[:, h % G, t:t + 1], bank[:, 0:n], AX.X, ALU.max,
                                            negate=True).then_inc(max_done.sem, 1)

            def shift(B, g):
                max_done.wait(dve, B, G * g + G - 1, T - 1)
                if g or B.n:
                    turn_full.wait(dve, B + (0 if g else -1), "sh", (g - 1) % NG)
                nm = neg_max[:, :, :].rearrange("p h t -> p (h t)")
                nc.vector.tensor_copy(shift_parts[:, 0, :], nm).then_inc(shift_high.sem, 1)
                shift_high.wait(dve, B, g)
                nc.vector.tensor_tensor(shift_parts[:, 1, :], nm, shift_parts[:, 0, :],
                                        ALU.subtract).then_inc(shift_ready.sem, 1)

            def extra_max(B, g):
                sm_full.wait(dve, B, "extra", g)
                if g or B.n:
                    xmax_exp.wait(dve, B + (0 if g else -1), (g - 1) % NG)
                bank = sm[sm_full.position(B, "extra", g) % 2]
                nc.vector.tensor_reduce(x_neg_max[:, :], bank[:, :], AX.X, ALU.max, negate=True).then_inc(max_done.sem, 1)

            def take_output(B, g):
                pv_done.wait(dve, B, G * g + G - 1)
                nc.vector.reciprocal(inv_sum[:, :, :], o_main[:, :, :, DH]).then_inc(o_inv.sem, 1)
                if B.n >= 2 or B.turn is not None:
                    turn_full.wait(dve, B + (-2), "ot", 1)
                o_inv.wait(dve, B, g)
                dst = att[B.n % 2][:, :, G * DH * g:G * DH * (g + 1)]
                split = STAGES[B.s] == SPLIT
                for h in range(G):
                    last = nc.vector.tensor_tensor(dst[:, :, DH * h:DH * (h + 1)], o_main[:, h, :, 0:DH],
                                                   inv_sum[:, h, :].unsqueeze(2).broadcast_to([P, T, DH]), ALU.mult)
                if not split:
                    last.then_inc(o_read.sem, 1)
                    dve.sem_inc(extra_steps.sem, 4)
                    return
                nc.vector.reciprocal(x_inv[0:REG, :], o_extra[0:REG, :, DH]).then_inc(extra_steps.sem, 1)
                extra_steps.wait(dve, B, g, 0)
                nc.vector.tensor_scalar(x_half[0:REG, :], x_inv[0:REG, :], 0.5, None, ALU.mult).then_inc(extra_steps.sem, 1)
                extra_steps.wait(dve, B, g, 1)
                nc.vector.tensor_tensor(x_out[0:REG, :, :], o_extra[0:REG, :, 0:DH],
                                        x_half[0:REG, :].unsqueeze(2).broadcast_to([REG, G, DH]), ALU.mult).then_inc(extra_steps.sem, 1)
                extra_steps.wait(dve, B, g, 2)
                reg = dst[0:REG, 0, :]
                nc.vector.scalar_tensor_tensor(out=reg, in0=reg, scalar=0.5,
                                               in1=x_out[0:REG, :, :].rearrange("p h c -> p (h c)"),
                                               op0=ALU.mult, op1=ALU.add).then_inc(o_read.sem, 1)
                dve.sem_inc(extra_steps.sem, 1)

            def take_turn(B, k, i):
                kind = STAGES[B.s]
                if B.turn is None and B.n < 0:
                    turn_full.wait_earlier(dve, B, 0, k, i)
                    dve.sem_inc(turn_free.sem, 1)
                elif k == "v" and kind == CAUSAL:
                    turn_full.wait(dve, B, k, i)
                    if B.n >= 2 or B.turn is not None:
                        pv_done.wait(dve, B + (-2), H - 1)
                    for t in range(2):
                        last = nc.vector.tensor_tensor(
                            values[B.n % 2][:, 2 * i + t, :, 0:DH],
                            turn_ps[:, D * t:D * (t + 1)].rearrange("p (h c) -> p h c", h=H),
                            v_bias[:, :].rearrange("p (h c) -> p h c", h=H), ALU.add)
                    last.then_inc(turn_free.sem, 1)
                elif k == "sh":
                    turn_full.wait(dve, B, k, i)
                    if i or B.n:
                        shift_in.wait(dve, B + (0 if i else -1), (i - 1) % NG)
                    nc.vector.tensor_copy(shift_rows[:, :], turn_b[0:2 * G * T, :]).then_inc(turn_free.sem, 1)
                elif k == "ot":
                    turn_full.wait(dve, B, k, i)
                    nc.vector.tensor_copy(att_t[:, i, :], turn_ps[:, :]).then_inc(turn_free.sem, 1)
                elif k == "out":
                    turn_full.wait(dve, B, k, i)
                    res_biased.wait(dve, B)
                    half = x_res[:, 2 * i:2 * i + 2, :].rearrange("p t d -> p (t d)")
                    nc.vector.tensor_tensor(half, turn_ps[:, :], half, ALU.add).then_inc(turn_free.sem, 1)
                    dve.wait_ge(turn_free.sem, turn_free.after(B, k, i))
                    dve.sem_inc(res_done.sem, 1)

            def first(B):
                statistics(B)
                if STAGES[B.s] == CAUSAL:
                    take_turn(B, "v", 0)
                    take_turn(B, "v", 1)
                for h in range(AHEAD):
                    maxima(B, h)
                    if h == G - 1:
                        shift(B, 0)
                take_turn(B, "sh", 0)
                register_queries(B)

            def body(B):
                kind = STAGES[B.s]
                if B.n + 1 < NB:
                    statistics(B + 1)
                for slot in range(H):
                    m = max_head(B.n, slot)
                    if m:
                        maxima(B + m[0], m[1])
                    if kind == SPLIT and slot % G == 1:
                        extra_max(B, slot // G)
                    if m and m[1] % G == G - 1:
                        shift(B + m[0], m[1] // G)
                    if slot % G == 0:
                        if slot:
                            take_output(B, slot // G - 1)
                        elif B.n:
                            take_output(B + (-1), NG - 1)
                    for k, off, i in turns_of(kind, B.n, slot):
                        take_turn(B + off, k, i)
                if B.n + 1 < NB:
                    register_queries(B + 1)

            def finish(B):
                take_output(B, NG - 1)
                for k, i in FINISH:
                    take_turn(B, k, i)

            n_class = 0
            n_clear = 0
            for s, kind in enumerate(STAGES):
                if s:
                    stage_start(dve, s)
                if kind == ROTARY:
                    for i in range(2):
                        nc.vector.memset(q_stack[i][MASK:MASK + 2, :, :], 0.0).then_inc(masks_cleared, 1)
                if kind == SPLIT:
                    base = NB * n_class
                    if n_class == 0:
                        nc.vector.tensor_tensor(prod[:, 0, :], guide[:, :], guide[:, :], ALU.mult).then_inc(g_step, 1)
                        dve.wait_ge(g_step, 1)
                        nc.vector.tensor_reduce(norms[:, H:2 * H], prod[:, 0, :].rearrange("p (h c) -> p h c", h=H),
                                                AX.X, ALU.add).then_inc(g_step, 1)
                        dve.wait_ge(g_step, 3)
                        nc.vector.tensor_tensor(guide[:, :].rearrange("p (h c) -> p h c", h=H),
                                                guide[:, :].rearrange("p (h c) -> p h c", h=H),
                                                norms[:, 0:H].unsqueeze(2).broadcast_to([P, H, DH]), ALU.mult).then_inc(g_step, 1)
                        dve.wait_ge(g_step, 4)
                    def class_batch(b, base=base):
                        dve.wait_ge(c_x, b * 16 + 16 * (base + 1))
                        for t in range(T):
                            last = nc.vector.bn_stats(bn[:, t, :], x_new[:, 0, t, :])
                        last.then_inc(c_bn, 1)
                        wait_before(dve, c_xn, b, base)
                        wait_reg(dve, c_bn, b + (base + 1), still)
                        for t in range(T):
                            last = nc.vector.bn_aggr(mean_var[:, t, :], bn[:, t, :])
                        last.then_inc(c_stats, 1)
                        dve.wait_ge(c_q, b + (base + 1))
                        for t in range(T):
                            last = nc.vector.tensor_tensor(prod[:, t, :], st[0][:, D * t:D * (t + 1)], guide[:, :], ALU.mult)
                        last.then_inc(c_prod, 1)
                        dve.wait_ge(c_prod, b + (base + 1))
                        nc.vector.tensor_reduce(dots[:, :], prod.rearrange("p t (h c) -> p (t h) c", h=H),
                                                AX.X, ALU.add).then_inc(c_dots, 1)
                        dve.wait_ge(c_sq, b + (base + 1))
                        nc.vector.tensor_reduce(norms[:, :], square.rearrange("p t (h c) -> p (t h) c", h=H),
                                                AX.X, ALU.add).then_inc(c_norm, 1)
                        dve.wait_ge(c_inv, b + (base + 1))
                        nc.vector.tensor_tensor(dots[:, :], dots[:, :], cosines[:, :], ALU.mult).then_inc(c_cos, 1)
                        dve.wait_ge(c_cos, b + (base + 1))
                        nc.vector.tensor_reduce(sim_b[:, :], dots[:, :].rearrange("p (t h) -> p t h", h=H),
                                                AX.X, ALU.add).then_inc(c_simb, 1)
                        dve.wait_ge(c_simb, b + (base + 1))
                        nc.vector.tensor_scalar(sim[:, bass.ds(b * T, T)], sim_b[:, :], 1.0 / H, None, ALU.mult).then_inc(c_sim, 1)

                    over_batches(dve, class_batch)
                    steps = [0]

                    def link(ins):
                        steps[0] += 1
                        ins.then_inc(c_step, 1)
                        dve.wait_ge(c_step, STEPS * n_class + steps[0])

                    STEPS = 15
                    dve.wait_ge(c_sim, NB * (n_class + 1))
                    link(nc.vector.tensor_tensor(cls[:, 0, :], sim[:, :], reg_big[:, :], ALU.add))
                    link(nc.vector.tensor_reduce(spread[:, 0:1], cls[:, 0, :], AX.X, ALU.min))
                    link(nc.vector.tensor_tensor(cls[:, 1, :], sim[:, :], reg_big[:, :], ALU.subtract))
                    link(nc.vector.tensor_scalar(extremes[:, 0:1], spread[:, 0:1], -1.0, None, ALU.mult))
                    nc.vector.tensor_reduce(extremes[:, 1:2], cls[:, 1, :], AX.X, ALU.max).then_inc(c_ext, 1)
                    dve.wait_ge(c_all, n_class + 1)
                    link(nc.vector.tensor_tensor(spread[:, 0:1], all_extremes[:, 1:2], all_extremes[:, 0:1], ALU.add))
                    link(nc.vector.reciprocal(spread[:, 1:2], spread[:, 0:1]))
                    link(nc.vector.tensor_scalar(cls[:, 0, :], sim[:, :], all_extremes[:, 0:1], spread[:, 1:2],
                                                 ALU.add, ALU.mult))
                    link(nc.vector.tensor_scalar(cls[:, 1, :], cls[:, 0, :], 0.9, None, ALU.is_gt))
                    link(nc.vector.tensor_scalar(cls[:, 2, :], reg_big[:, :], 0.0, None, ALU.is_gt))
                    link(nc.vector.tensor_tensor(cls[:, 0, :], cls[:, 1, :], cls[:, 2, :], ALU.max))
                    link(nc.vector.tensor_copy(class_rows[:, 0, :], cls[:, 0, :]))
                    link(nc.vector.tensor_scalar(class_rows[:, 1, :], cls[:, 0, :], -1.0, 1.0, ALU.mult, ALU.add))
                    link(nc.vector.tensor_scalar(class_rows[:, 2, :], cls[:, 0, :], BIG, -BIG, ALU.mult, ALU.add))
                    link(nc.vector.tensor_tensor(cls[:, 0, :], cls[:, 0, :], cls[:, 2, :], ALU.subtract))
                    link(nc.vector.tensor_scalar(class_rows[:, 3, :], cls[:, 0, :], -BIG, None, ALU.mult))
                    assert steps[0] == STEPS
                    dve.sem_inc(c_rows, 1)
                    dve.wait_ge(c_rt, n_class + 1)
                    nc.vector.tensor_copy(class_t[:, 0, :], turn_b)
                    nc.vector.tensor_copy(class_t[:, 1, :], turn_b2).then_inc(c_rtc, 1)
                    n_class += 1
                run_stage(dve, s, first, body, finish)

        @block.scalar
        def _(act):
            stage_start(act, 0)
            nc.scalar.mul(q_bias[:, :], qk_bias[:, 0:KT], DH ** -0.5).then_inc(masks_cleared, 1)

            def exponentials(B, h):
                kind = STAGES[B.s]
                for c in range(2):
                    st_full.wait(act, B, h, c)
                    if h >= 2 or B.n:
                        pv_done.wait(act, B + (0 if h >= 2 else -1), (h - 2) % H)
                    off = prob_offset(kind, 2 * c)
                    n = prob_offset(kind, 2 * c + 1) - off + L - key_start(kind, 2 * c + 1)
                    nc.scalar.activation(probs[h % 2][:, off:off + n], st[c][:, 0:n], ACT.Exp).then_inc(exp_done.sem, 1)

            def extra_exp(B, g):
                max_done.wait(act, B, "extra", g)
                if g or B.n:
                    turn_full.wait(act, B + (0 if g else -1), "ex", (g - 1) % NG)
                bank = sm[sm_full.position(B, "extra", g) % 2]
                nc.scalar.activation(x_probs[:, :], bank[:, :], ACT.Exp, bias=x_neg_max[:, :]).then_inc(xmax_exp.sem, 1)

            def take_turn(B, k, i):
                kind = STAGES[B.s]
                if k == "xt":
                    turn_full.wait(act, B, k, i)
                    nc.scalar.copy(xn_t[:, i, :], turn_ps[:, :]).then_inc(turn_free.sem, 1)
                elif k == "qk":
                    turn_full.wait(act, B, k, i)
                    if B.n:
                        split_steps.wait(act, B + (-1), 3 if i > 1 else 1, 3)
                    scale = DH ** -0.5 if i < 2 else 1.0
                    if kind == CAUSAL:
                        bias = q_bias[:, i:i + 1] if i < 2 else qk_bias[:, i:i + 1]
                        nc.scalar.activation(qk_f[:, i, :], turn_ps[:, :], ACT.Identity, bias=bias,
                                             scale=scale).then_inc(turn_free.sem, 1)
                    else:
                        nc.scalar.activation(qk_f[:, i, :], turn_ps[:, :], ACT.Copy, scale=scale).then_inc(turn_free.sem, 1)
                elif k == "v" and kind != CAUSAL:
                    turn_full.wait(act, B, k, i)
                    if B.n >= 2 or B.turn is not None:
                        pv_done.wait(act, B + (-2), H - 1)
                    for t in range(2):
                        last = nc.scalar.copy(values[B.n % 2][:, 2 * i + t, :, 0:DH],
                                              turn_ps[:, D * t:D * (t + 1)].rearrange("p (h c) -> p h c", h=H))
                    last.then_inc(turn_free.sem, 1)
                elif k == "ex":
                    turn_full.wait(act, B, k, i)
                    if i or B.n:
                        pv_done.wait(act, B + (0 if i else -1), G * ((i - 1) % NG) + 2)
                    nc.scalar.copy(x_probs_t[:, :, :].rearrange("p t c -> p (t c)"), turn_ps[:, :]).then_inc(turn_free.sem, 1)

            def first(B):
                if B.s == 0:
                    act.wait_ge(masks_cleared, 1)
                for k, i in PREPARE:
                    take_turn(B, k, i)

            def body(B):
                kind = STAGES[B.s]
                for slot in range(H):
                    if kind == SPLIT and slot % G == 2:
                        extra_exp(B, slot // G)
                    exponentials(B, slot)
                    for k, off, i in turns_of(kind, B.n, slot):
                        take_turn(B + off, k, i)

            n_class = 0
            for s, kind in enumerate(STAGES):
                if s:
                    stage_start(act, s)
                if kind == SPLIT:
                    base = NB * n_class
                    def class_batch(b, base=base):
                        act.wait_ge(c_tr, b + (base + 1))
                        nc.scalar.copy(xn_t[:, :, :].rearrange("p k t -> p (k t)"), st[1][:, :]).then_inc(c_trc, 1)
                        act.wait_ge(c_prod, b + (base + 1))
                        wait_before(act, c_norm, b, base)
                        nc.scalar.activation(square.rearrange("p t d -> p (t d)"), st[0][:, :], ACT.Square).then_inc(c_sq, 1)

                    over_batches(act, class_batch)
                    n_class += 1
                run_stage(act, s, first, body, nothing)

        @block.tensor
        def _(pe):
            stage_start(pe, 0)

            def score_rows(kind, shifted):
                return ROWS if shifted else (SHIFT if kind == SPLIT else PARTS)

            def max_tiles(B, h, slot_in_group):
                kind = STAGES[B.s]
                q_in.wait(pe, B)
                k_in.wait(pe, B)
                r = score_rows(kind, False)
                q, k = q_stack[B.n % 2], k_stack[B.n % 2]
                for t in range(T):
                    max_done.wait_earlier(pe, B, 2, h, t)
                    if t == 1 and slot_in_group is not None:
                        xmax_exp.wait(pe, *slot_in_group)
                    n = (t + 1) * P if kind == CAUSAL else L
                    bank = sm[sm_full.position(B, h, t) % 2]
                    last = nc.tensor.matmul(bank[:, 0:n], q[0:r, h, t * P:(t + 1) * P], k[0:r, h, 0:n],
                                            start=True, stop=kind != CAUSAL)
                    if kind == CAUSAL:
                        last = nc.tensor.matmul(bank[:, t * P:(t + 1) * P], ident_b[:, :], causal_qk[:, :],
                                                start=False, stop=True)
                    last.then_inc(sm_full.sem, 1)

            def extra_tile(B, g):
                qx_done.wait(pe, B)
                max_done.wait_earlier(pe, B, 2, "extra", g)
                bank = sm[sm_full.position(B, "extra", g) % 2]
                for i in range(G):
                    h = G * g + i
                    last = nc.tensor.matmul(bank[XW * i:XW * (i + 1), :], qx[B.n % 2][0:SHIFT, h, :],
                                            k_stack[B.n % 2][0:SHIFT, h, :], start=True, stop=True)
                last.then_inc(sm_full.sem, 1)

            def scores_t(B, h):
                kind = STAGES[B.s]
                if h % G == 0:
                    shift_in.wait(pe, B, h // G)
                if kind == ROTARY and B.n == 0 and h == 0:
                    pe.wait_ge(masks_cleared, 3)
                q, k = q_stack[B.n % 2], k_stack[B.n % 2]
                for c in range(2):
                    if h or B.n:
                        exp_done.wait(pe, B + (0 if h else -1), (h - 1) % H, c)
                    for kt in (2 * c, 2 * c + 1):
                        q0 = key_start(kind, kt)
                        off = prob_offset(kind, kt) - prob_offset(kind, 2 * c)
                        last = nc.tensor.matmul(st[c][:, off:off + L - q0], k[0:ROWS, h, kt * P:(kt + 1) * P],
                                                q[0:ROWS, h, q0:L], start=True, stop=kind != CAUSAL)
                        if kind == CAUSAL:
                            last = nc.tensor.matmul(st[c][:, off:off + P], ident_b[:, :], causal_kq[:, :],
                                                    start=False, stop=True)
                    last.then_inc(st_full.sem, 1)

            def extra_outputs(B, g):
                turn_free.wait(pe, B, "ex", g)
                for i in range(G):
                    for kt in range(T):
                        nc.tensor.matmul(o_extra[0:8, i, :], x_probs_t[:, kt, XW * i:XW * i + 8],
                                         values[B.n % 2][:, kt, G * g + i, :], start=kt == 0, stop=kt == T - 1)

            def outputs(B, h):
                kind = STAGES[B.s]
                exp_done.wait(pe, B, h, 1)
                if h == 0:
                    turn_free.wait(pe, B, "v", 1)
                if h % G == 0 and (h or B.n):
                    o_read.wait(pe, B + (0 if h else -1), (h // G - 1) % NG)
                for t in range(T):
                    keys = range(t + 1) if kind == CAUSAL else range(T)
                    for kt in keys:
                        col = prob_offset(kind, kt) + t * P - key_start(kind, kt)
                        last = nc.tensor.matmul(o_main[:, h % G, t, :], probs[h % 2][:, col:col + P],
                                                values[B.n % 2][:, kt, h, :], start=kt == 0, stop=kt == keys[-1])
                last.then_inc(pv_done.sem, 1)

            def turn(B, k, i):
                kind = STAGES[B.s]
                if B.turn is None and B.n < 0:
                    turn_free.wait_earlier(pe, B, 1, k, i)
                    pe.sem_inc(turn_full.sem, 1)
                    return
                if k == "xt":
                    xn_done.wait(pe, B)
                elif k == "sh":
                    shift_ready.wait(pe, B, i)
                elif k == "ex":
                    xmax_exp.wait(pe, B, i)
                elif k == "ot":
                    o_read.wait(pe, B, NG - 1)
                turn_free.wait_earlier(pe, B, 1, k, i)
                if k == "xt":
                    for t in range(T):
                        last = nc.tensor.transpose(turn_ps[:, t * P:(t + 1) * P], xn[:, t, i * P:(i + 1) * P], ident[:, :])
                elif k == "qk":
                    weight = (wq if i < 2 else wk)[kind]
                    m = i % 2
                    for kt in range(KT):
                        last = nc.tensor.matmul(turn_ps[:, :], weight[:, kt, m * P:(m + 1) * P], xn_t[:, kt, :],
                                                start=kt == 0, stop=kt == KT - 1)
                elif k == "v":
                    for j in range(2):
                        t = 2 * i + j
                        for kt in range(KT):
                            last = nc.tensor.matmul(turn_ps[:, j * D:(j + 1) * D], xn_t[:, kt, t * P:(t + 1) * P],
                                                    wv[kind][:, kt, :], start=kt == 0, stop=kt == KT - 1)
                elif k == "sh":
                    last = nc.tensor.transpose(turn_b[0:2 * G * T, :],
                                               shift_parts[:, :, :].rearrange("p a c -> p (a c)"), ident_b[:, :])
                elif k == "ex":
                    for t in range(T):
                        last = nc.tensor.transpose(turn_ps[:, t * P:(t + 1) * P], x_probs[:, t * P:(t + 1) * P], ident[:, :])
                elif k == "ot":
                    for t in range(T):
                        last = nc.tensor.transpose(turn_ps[:, t * P:(t + 1) * P], att[B.n % 2][:, t, i * P:(i + 1) * P], ident[:, :])
                elif k == "out":
                    for j in range(2):
                        t = 2 * i + j
                        for kt in range(KT):
                            last = nc.tensor.matmul(turn_ps[:, j * D:(j + 1) * D], att_t[:, kt, t * P:(t + 1) * P],
                                                    wo[kind][:, kt, :], start=kt == 0, stop=kt == KT - 1)
                last.then_inc(turn_full.sem, 1)

            def first(B):
                for k, i in PREPARE:
                    turn(B, k, i)
                for h in range(AHEAD):
                    max_tiles(B, h, None)
                turn(B, "sh", 0)

            def body(B):
                kind = STAGES[B.s]
                for slot in range(H):
                    scores_t(B, slot)
                    m = max_head(B.n, slot)
                    if m:
                        max_tiles(B + m[0], m[1], (B, slot // G) if kind == SPLIT and slot % G == 2 else None)
                    if kind == SPLIT and slot % G == 1:
                        extra_tile(B, slot // G)
                    if kind == SPLIT and slot % G == 3:
                        extra_outputs(B, slot // G)
                    if slot:
                        outputs(B, slot - 1)
                    elif B.n:
                        outputs(B + (-1), H - 1)
                    for k, off, i in turns_of(kind, B.n, slot):
                        turn(B + off, k, i)

            def finish(B):
                outputs(B, H - 1)
                for k, i in FINISH:
                    turn(B, k, i)

            n_class = 0
            for s, kind in enumerate(STAGES):
                if s:
                    stage_start(pe, s)
                if kind == SPLIT:
                    base = NB * n_class
                    def class_batch(b, base=base):
                        pe.wait_ge(c_xn, b + (base + 1))
                        wait_before(pe, c_trc, b, base)
                        for kt in range(KT):
                            for t in range(T):
                                last = nc.tensor.transpose(st[1][:, kt * L + t * P:kt * L + (t + 1) * P],
                                                           xn[:, t, kt * P:(kt + 1) * P], ident[:, :])
                        last.then_inc(c_tr, 1)
                        pe.wait_ge(c_trc, b + (base + 1))
                        wait_before(pe, c_prod, b, base)
                        wait_before(pe, c_sq, b, base)
                        for t in range(T):
                            for kt in range(KT):
                                last = nc.tensor.matmul(st[0][:, D * t:D * (t + 1)], xn_t[:, kt, t * P:(t + 1) * P],
                                                        wq_class[:, kt, :], start=kt == 0, stop=kt == KT - 1)
                        last.then_inc(c_q, 1)

                    over_batches(pe, class_batch)
                    pe.wait_ge(c_rows, n_class + 1)
                    rows = class_rows[:, :, :].rearrange("p k c -> p (k c)")
                    nc.tensor.transpose(turn_b, rows[:, 0:P], ident_b[:, :])
                    nc.tensor.transpose(turn_b2, rows[:, P:2 * P], ident_b[:, :]).then_inc(c_rt, 1)
                    n_class += 1
                run_stage(pe, s, first, body, finish)


def kernel(**inputs):
    import ml_dtypes
    import numpy as np
    import concourse.bacc as bacc
    from concourse.bass_utils import run_bass_kernel_spmd

    a = {k: np.asarray(v) for k, v in inputs.items()}

    def by_feature(m):
        return m.reshape(D, H, DH).transpose(0, 2, 1).reshape(D, D)

    def columns(v):
        return v.reshape(H, DH).transpose(1, 0).reshape(KT, P).transpose(1, 0)

    def on_all(v):
        return np.broadcast_to(v.reshape(1, D), (P, D))

    w = {}
    for kind, q, k, v, o in (
        (CAUSAL, a["L0_attn_a_Wq"].T, a["L0_attn_a_Wk"].T, a["L0_attn_a_Wv"].T, a["L0_attn_a_Wo"].T),
        (SPLIT, *np.split(a["L0_ffn_W_qkv"], 3, axis=1), a["L0_ffn_W_proj"]),
        (ROTARY, *np.split(a["L0_attn_b_Wqkv"], 3, axis=1), a["L0_attn_b_Wo"]),
    ):
        w[f"wq_{kind}"], w[f"wk_{kind}"], w[f"wv_{kind}"], w[f"wo_{kind}"] = by_feature(q), by_feature(k), v, o
        if kind == SPLIT:
            w["wq_class"] = q
    w["qk_bias"] = np.concatenate([columns(a["L0_attn_a_bq"]), columns(a["L0_attn_a_bk"])], axis=1)
    w["v_bias"] = on_all(a["L0_attn_a_bv"])
    w["o_bias_causal"] = on_all(a["L0_attn_a_bo"])
    w["o_bias_split"] = on_all(a["L0_ffn_b_proj"])
    w["guide"] = on_all(a["L0_ffn_g_info"][0, 0])

    freq = (1.0 / np.float32(10000.0) ** (np.arange(0, DH, 2, dtype=np.float32) / np.float32(DH))).astype(np.float32)
    angle = np.outer(freq, np.arange(L, dtype=np.float32)).astype(np.float32)
    later = np.arange(P)[:, None] > np.arange(P)[None, :]
    c = {
        "cos": np.repeat(np.cos(angle), H, axis=0).astype(np.float32),
        "sin": np.repeat(np.sin(angle), H, axis=0).astype(np.float32),
        "ident": np.eye(P, dtype=np.float32),
        "ident_b": np.eye(P).astype(ml_dtypes.bfloat16),
        "causal_kq": np.where(later, -BIG, 0.0).astype(ml_dtypes.bfloat16),
        "causal_qk": np.where(later.T, -BIG, 0.0).astype(ml_dtypes.bfloat16),
        "reg_big": np.where((np.arange(P)[:, None] < REG) & (np.arange(NB * T)[None, :] % T == 0), 1e30, 0.0).astype(np.float32),
        "neg_class": np.repeat(np.array([[0.0], [1.0]]), H * XW, axis=1).astype(ml_dtypes.bfloat16),
    }

    nc = bacc.Bacc("TRN2", target_bir_lowering=False, num_devices=1)
    arrays = {}

    def put(name, value):
        value = np.ascontiguousarray(value)
        arrays[name] = value
        return nc.dram_tensor(name, value.shape, mybir.dt.from_np(value.dtype), kind="ExternalInput").ap()

    x_in = put("x", a["L0_attn_a_x"])
    w = {n: put("w_" + n, v) for n, v in w.items()}
    c = {n: put("c_" + n, v) for n, v in c.items()}
    out = nc.dram_tensor("out", (NB, L, D), F32, kind="ExternalOutput").ap()
    hybrid_blocks(nc, x_in, w, c, out)
    result = run_bass_kernel_spmd(nc, [arrays], core_ids=[0])
    return result.results[0]["out"]
```

```python
from contextlib import ExitStack

import concourse.bass as bass
from concourse import mybir

F32 = mybir.dt.float32
BF16 = mybir.dt.bfloat16
ALU = mybir.AluOpType
ACT = mybir.ActivationFunctionType
AX = mybir.AxisListType

P = 128
NB = 16
L = 512
D = 256
H = 16
DH = D // H
T = L // P
KT = D // P
G = 4
NG = H // G
REG = 5
XW = 32
EPS = 1e-5
PARTS = 6 * DH
MASK = PARTS
SHIFT = PARTS + 2
ROWS = PARTS + 4
VW = 32
AHEAD = 6
BIG = float(2.0 ** 100)

CAUSAL, SPLIT, ROTARY = "causal", "split", "rotary"
STAGES = [CAUSAL, SPLIT, ROTARY, SPLIT]

Q_BLOCKS = [0, 0, 0, 1, 1, 2]
K_BLOCKS = [0, 1, 2, 0, 1, 0]

TURNS = {
    1: ([("xt", 1, 0)], [("xt", 1, 1)]),
    2: ([("sh", 0, 1)], [("og", -1, 3)]),
    3: ([("xo", -1, 3)], [("ex", 0, 0)]),
    4: ([("qk", 1, 0)], [("qk", 1, 1)]),
    5: ([("qk", 1, 2)], [("qk", 1, 3)]),
    6: ([("sh", 0, 2)], [("og", 0, 0)]),
    7: ([("xo", 0, 0)], [("ex", 0, 1)]),
    8: ([("v", 1, 0)], [("v", 1, 1)]),
    9: ([("ot", -1, 0)], [("ot", -1, 1)]),
    10: ([("sh", 0, 3)], [("og", 0, 1)]),
    11: ([("xo", 0, 1)], [("ex", 0, 2)]),
    12: ([("out", -1, 0)], []),
    13: ([("out", -1, 1)], []),
    14: ([("sh", 1, 0)], [("og", 0, 2)]),
    15: ([("xo", 0, 2)], [("ex", 0, 3)]),
}
PREPARE = [("xt", 0), ("xt", 1), ("qk", 0), ("qk", 1), ("qk", 2), ("qk", 3), ("v", 0), ("v", 1)]


def finish_turns(kind):
    return ([("og", 3)] + ([("xo", 3)] if kind == SPLIT else [])
            + [("ot", 0), ("ot", 1), ("out", 0), ("out", 1)])


def chunks_of(slot):
    g, c, pair = slot // G, slot % G // 2, slot % 2
    return [(G * g + 2 * pair + i, c) for i in range(2)]


def values_of(slot):
    n = slot - 2
    return (0, n // T, n % T) if n >= 0 else (-1, NG - 1, T + n)


def turns_of(kind, b, slot, place=None):
    first, second = TURNS.get(slot, ([], []))
    turns = first + second if place is None else (first, second)[place]
    return [t for t in turns if b + t[1] < NB and (t[0] not in ("ex", "xo") or kind == SPLIT)]


def max_head(b, slot):
    h = slot + AHEAD
    off, h = (0, h) if h < H else (1, h - H)
    return (off, h) if b + off < NB else None


def key_start(kind, kt):
    return kt * P if kind == CAUSAL else 0


def chunk_offset(kind, kt):
    return (L - key_start(kind, kt - 1)) if kt % 2 else 0


class Batch:

    def __init__(self, s, n, turn=None):
        self.s, self.n, self.turn = s, n, turn

    def __add__(self, k):
        return Batch(self.s, self.n + k, self.turn)

    def index(self):
        return self.n if self.turn is None else self.turn * 2 + self.n

    def one(self):
        return bass.ds(self.index(), 1)


LOOPS = (NB - 2) // 2


def over_batches(eng, body):
    body(0)
    with eng.Fori(1, NB, 1) as b:
        body(b)


def wait_before(eng, sem, b, base, still=None):
    if not isinstance(b, int) or b + base:
        wait_reg(eng, sem, b + base, still)


def wait_reg(eng, sem, value, still=None):
    eng.wait_ge(sem, value)
    if still is not None and not isinstance(value, int):
        eng.sem_inc(still, 1)


class Count:

    def __init__(self, sem, labels, step=1):
        self.sem, self.step = sem, step
        self.at = {lab: (i + 1) * step for i, lab in enumerate(labels)}
        assert len(self.at) == len(labels)

    def after(self, B, *label):
        lab = lambda n: (B.s, n) + label
        if B.turn is None:
            return self.at[lab(B.n)]
        second = self.at[lab(B.n + 2)]
        d = self.at[lab(B.n + 4)] - second
        c = second - d
        assert c > 0 and all(self.at.get(lab(B.n + 2 * i), c) == c + d * i for i in range(LOOPS))
        return B.turn * d + c

    def wait(self, eng, B, *label, still=None):
        if B.turn is None and B.n < 0:
            return
        wait_reg(eng, self.sem, self.after(B, *label), still)

    def wait_earlier(self, eng, B, back, *label):
        v = self.after(B, *label) - self.step * back
        if B.turn is None and v <= 0:
            return
        eng.wait_ge(self.sem, v)

    def position(self, B, *label):
        return self.at[(B.s, B.n) + label] // self.step - 1


def steps_of(per_body, first=None, last=None):
    out = []
    for s, kind in enumerate(STAGES):
        if first:
            out += [(s, 0) + lab for lab in first(kind)]
        for b in range(NB):
            out += [(s, b + off) + lab for off, lab in per_body(kind, b)]
        if last:
            out += [(s, NB - 1) + lab for lab in last(kind)]
    return out


def hybrid_blocks(nc, x_in, w, consts, out):
    ctx = ExitStack()
    with ctx:
        def sb(name, shape, dt=F32):
            return ctx.enter_context(nc.sbuf_tensor(name, shape, dt))

        def ps(name, shape):
            return ctx.enter_context(nc.psum_tensor(name, shape, F32))

        def sem(name):
            return ctx.enter_context(nc.semaphore(name))

        xs = [x_in] + [nc.dram_tensor(f"x_after_{s}", (NB, L, D), F32, kind="Internal").ap() for s in range(3)] + [out]
        q_stack_d = nc.dram_tensor("q_stack_d", (NB, SHIFT, H, L), BF16, kind="Internal").ap()
        k_stack_d = nc.dram_tensor("k_stack_d", (NB, SHIFT, H, L), BF16, kind="Internal").ap()
        mask_d = nc.dram_tensor("mask_d", (4, NB * L), BF16, kind="Internal").ap()

        wq = {k: sb(f"wq_{k}", [P, KT, D]) for k in (CAUSAL, SPLIT)}
        wk = {k: sb(f"wk_{k}", [P, KT, D]) for k in (CAUSAL, SPLIT)}
        wv = {k: sb(f"wv_{k}", [P, KT, D]) for k in (CAUSAL, SPLIT)}
        wo = {k: sb(f"wo_{k}", [P, KT, D]) for k in (CAUSAL, SPLIT)}
        for tile in (wq, wk, wv, wo):
            tile[ROTARY] = tile[CAUSAL]
        wq_class = sb("wq_class", [P, KT, D])
        qk_bias = sb("qk_bias", [P, 2 * KT])
        q_bias = sb("q_bias", [P, KT])
        v_bias = sb("v_bias", [P, D])
        o_bias = {CAUSAL: sb("o_bias_c", [P, D]), SPLIT: sb("o_bias_s", [P, D])}
        cos_t = sb("cos_t", [P, L])
        sin_t = sb("sin_t", [P, L])
        ident = sb("ident", [P, P])
        ident_b = sb("ident_b", [P, P], BF16)
        causal_kq = sb("causal_kq", [P, P], BF16)
        causal_qk = sb("causal_qk", [P, P], BF16)
        guide = sb("guide", [P, D])
        minus_half = sb("minus_half", [P, T * H])
        reg_big = sb("reg_big", [P, NB * T])

        x_new = sb("x_new", [P, T, D])
        bn = sb("bn", [P, T, 6])
        mean_var = sb("mean_var", [P, T, 2])
        var_eps = sb("var_eps", [P, T])
        rstd = sb("rstd", [P, T])
        xn = sb("xn", [P, T, D])
        xn_t = sb("xn_t", [P, KT, L])
        qk_f = sb("qk_f", [P, 4, L])
        rot_f = sb("rot_f", [P, KT, L])
        rest = sb("rest", [P, L])
        parts = sb("parts", [P, 4, 3, L], BF16)
        q_stack = [sb(f"q_stack{i}", [P, H, L], BF16) for i in range(2)]
        k_stack = [sb(f"k_stack{i}", [P, H, L], BF16) for i in range(2)]
        qx = [sb(f"qx{i}", [P, H, XW], BF16) for i in range(2)]
        values = [sb(f"values{i}", [P, T, H, VW]) for i in range(2)]
        neg_max = sb("neg_max", [P, G, T])
        shift_parts = sb("shift_parts", [P, 2, G * T], BF16)
        shift_rows = sb("shift_rows", [2 * G * T, P], BF16)
        probs = [sb(f"probs{i}", [P, G, 2 * L]) for i in range(2)]
        x_neg_max = sb("x_neg_max", [P, 1])
        x_probs = sb("x_probs", [P, L])
        x_probs_t = sb("x_probs_t", [P, T, P])
        rot_a = x_probs[:, :]
        rot_b = x_probs_t[:, :, :].rearrange("p t c -> p (t c)")
        out_sums = sb("out_sums", [P, L])
        inv_sum = sb("inv_sum", [P, T * G])
        x_inv = sb("x_inv", [P, G])
        x_half = sb("x_half", [P, G])
        x_out = sb("x_out", [P, G, DH])
        att = [sb(f"att{i}", [P, T, D]) for i in range(2)]
        att_t = sb("att_t", [P, KT, L])
        x_res = sb("x_res", [P, T, D])

        prod = probs[0][:, 0, :].rearrange("p (t d) -> p t d", t=T)
        square = probs[1][:, 0, :].rearrange("p (t d) -> p t d", t=T)
        dots = sb("dots", [P, T * H])
        norms = sb("norms", [P, T * H])
        cosines = sb("cosines", [P, T * H])
        sim_b = sb("sim_b", [P, T])
        sim = sb("sim", [P, NB * T])
        extremes = sb("extremes", [P, 2])
        all_extremes = sb("all_extremes", [P, 2])
        spread = sb("spread", [P, 2])
        cls = sb("cls", [P, 3, NB * T])
        class_rows = sb("class_rows", [P, 4, NB * T], BF16)
        class_t = sb("class_t", [P, 2, P], BF16)

        st = [ps(f"scores_t{i}", [P, 2 * L]) for i in range(2)]
        sm = [ps(f"scores{i}", [P, L]) for i in range(2)]
        o_ps = ps("o_ps", [P, L])
        turn_ps = ps("turn_ps", [P, L])
        turn_heads = turn_ps[:, :].rearrange("p (a c) -> p a c", c=VW)
        turn_b = turn_ps[:, 0:P // 2].bitcast(BF16)
        turn_b2 = turn_ps[:, P // 2:P].bitcast(BF16)

        def turn_steps(kind, b):
            return [(off, (k, i)) for slot in range(H) for k, off, i in turns_of(kind, b, slot)]

        turn_args = (turn_steps, lambda kind: PREPARE + [("sh", 0)], finish_turns)
        turn_full = Count(sem("turn_full"), steps_of(*turn_args))
        turn_free = Count(sem("turn_free"), steps_of(*turn_args))

        def max_steps(kind, b):
            res = []
            for slot in range(H):
                m = max_head(b, slot)
                if m:
                    res += [(m[0], (m[1], t)) for t in range(T)]
                if kind == SPLIT and slot % G == 1:
                    res.append((0, ("extra", slot // G)))
            return res

        max_args = (max_steps, lambda kind: [(h, t) for h in range(AHEAD) for t in range(T)])
        sm_full = Count(sem("scores_full"), steps_of(*max_args))
        max_done = Count(sem("max_done"), steps_of(*max_args))

        chunks = (lambda kind, b: [(0, lab) for slot in range(H) for lab in chunks_of(slot)],)
        groups = (lambda kind, b: [(0, (g,)) for g in range(NG)],)
        tiles = (lambda kind, b: [(0, (g, kt)) for g in range(NG) for kt in range(T)],)
        st_full = Count(sem("scores_t_full"), steps_of(*chunks))
        exp_done = Count(sem("exp_done"), steps_of(*chunks))
        pv_done = Count(sem("pv_done"), steps_of(*tiles))
        o_taken = Count(sem("o_taken"), steps_of(*groups))
        o_inv = Count(sem("o_inv"), steps_of(*groups))
        o_scaled = Count(sem("o_scaled"), steps_of(*groups))

        def per_group_shift(kind, b):
            return [(off, (i,)) for slot in range(H) for k, off, i in turns_of(kind, b, slot) if k == "sh"]

        shift_args = (per_group_shift, lambda kind: [(0,)])
        shift_high = Count(sem("shift_high"), steps_of(*shift_args))
        shift_ready = Count(sem("shift_ready"), steps_of(*shift_args))
        shift_in = Count(sem("shift_in"), steps_of(*shift_args), 16)

        nexts = (lambda kind, b: [(1, ())] if b + 1 < NB else [], lambda kind: [()])
        x_loaded = Count(sem("x_loaded"), steps_of(*nexts), 16)
        bn_done = Count(sem("bn_done"), steps_of(*nexts))
        stats_done = Count(sem("stats_done"), steps_of(*nexts))
        eps_done = Count(sem("eps_done"), steps_of(*nexts))
        rstd_done = Count(sem("rstd_done"), steps_of(*nexts))
        xn_done = Count(sem("xn_done"), steps_of(*nexts))
        qx_done = Count(sem("qx_done"), steps_of(*nexts))
        q_in = Count(sem("q_in"), steps_of(*nexts), 16)
        k_in = Count(sem("k_in"), steps_of(*nexts), 16)

        def of_next(items):
            return (lambda kind, b: [(1, i) for i in items] if b + 1 < NB else [], lambda kind: list(items))

        split_steps = Count(sem("split_steps"), steps_of(*of_next([(j, i) for j in range(4) for i in range(4)])))
        rot_steps = Count(sem("rot_steps"), steps_of(*of_next([(j, i) for j in range(4) for i in range(3)])))
        parts_out = Count(sem("parts_out"), steps_of(*of_next([(j, i) for j in range(4) for i in range(6)])), 16)

        prevs = (lambda kind, b: [(-1, ())] if b else [], None, lambda kind: [()])
        res_loaded = Count(sem("res_loaded"), steps_of(*prevs), 16)
        res_biased = Count(sem("res_biased"), steps_of(*prevs))
        res_halves = (lambda kind, b: [(-1, (v,)) for v in range(2)] if b else [], None, lambda kind: [(0,), (1,)])
        res_done = Count(sem("res_done"), steps_of(*res_halves))
        stored = Count(sem("stored"), steps_of(lambda kind, b: [(-1, ())], None, lambda kind: [()]), 16)

        xmax_exp = Count(sem("extra_exp"), steps_of(lambda kind, b: [(0, (g,)) for g in range(NG)] if kind == SPLIT else []))
        extra_steps = Count(sem("extra_steps"), steps_of(
            lambda kind, b: [(0, (g, i)) for g in range(NG) for i in range(4)] if kind == SPLIT else []))

        consts_in = sem("consts_in")
        preset = sem("preset")
        masks_cleared = sem("masks_cleared")
        rotary_in = sem("rotary_in")
        c_x = sem("c_x"); c_bn = sem("c_bn"); c_stats = sem("c_stats"); c_eps = sem("c_eps")
        c_rstd = sem("c_rstd"); c_xn = sem("c_xn"); c_tr = sem("c_tr"); c_trc = sem("c_trc")
        c_q = sem("c_q"); c_prod = sem("c_prod"); c_sq = sem("c_sq"); c_dots = sem("c_dots")
        c_norm = sem("c_norm"); c_inv = sem("c_inv"); c_cos = sem("c_cos"); c_simb = sem("c_simb")
        c_sim = sem("c_sim"); c_ext = sem("c_ext"); c_all = sem("c_all"); c_step = sem("c_step")
        c_rows = sem("c_rows"); c_rt = sem("c_rt"); c_rtc = sem("c_rtc"); c_dram = sem("c_dram")
        c_masks = sem("c_masks"); g_step = sem("g_step")

        still = sem("passed")

        block = ctx.enter_context(nc.Block())

        def run_stage(eng, s, first, body, finish):
            first(Batch(s, 0))
            body(Batch(s, 0))
            with eng.Fori(0, LOOPS, 1) as i:
                body(Batch(s, 1, i))
                body(Batch(s, 2, i))
            body(Batch(s, NB - 1))
            finish(Batch(s, NB - 1))

        def stage_start(eng, s):
            if s:
                eng.wait_ge(stored.sem, 16 * (NB + 1) * s)
            else:
                eng.wait_ge(consts_in, 16 * len(loads))
                eng.wait_ge(preset, PRESETS)

        nothing = lambda B: None

        loads = []
        weights = {k: [(tile[k][:, :, :], w[f"{name}_{k}"].rearrange("(k p) n -> p k n", p=P))
                       for tile, name in ((wq, "wq"), (wk, "wk"), (wv, "wv"), (wo, "wo"))]
                   for k in (CAUSAL, SPLIT, ROTARY)}
        loads += weights[CAUSAL] + weights[SPLIT]
        loads.append((wq_class[:, :, :], w["wq_class"].rearrange("(k p) n -> p k n", p=P)))
        for tile, name in ((qk_bias, "qk_bias"), (v_bias, "v_bias"), (o_bias[CAUSAL], "o_bias_causal"),
                           (o_bias[SPLIT], "o_bias_split"), (guide, "guide")):
            loads.append((tile[:, :], w[name]))
        for tile, name in ((cos_t, "cos"), (sin_t, "sin"), (ident, "ident"), (ident_b, "ident_b"),
                           (causal_kq, "causal_kq"), (causal_qk, "causal_qk"), (reg_big, "reg_big")):
            loads.append((tile[:, :], consts[name]))
        for i in range(2):
            loads.append((qx[i][MASK:MASK + 2, :, :].rearrange("p h c -> p (h c)"), consts["neg_class"]))
        PRESETS = 5 * 2 + 1 + 2
        QX_ROWS = PARTS

        @block.sync
        def _(sp):
            for dst, src in loads:
                sp.dma_start(dst, src).then_inc(consts_in, 16)
            stage_start(sp, 0)

            def load_x(B):
                xn_done.wait(sp, B + (-1), still=still)
                sp.dma_start(x_new[:, :, :],
                             xs[B.s][B.one()].rearrange("a (t p) d -> p (a t) d", p=P)).then_inc(x_loaded.sem, 16)

            def load_stack(B, q):
                kind = STAGES[B.s]
                tile, dram, blocks, here = ((q_stack, q_stack_d, Q_BLOCKS, q_in) if q
                                            else (k_stack, k_stack_d, K_BLOCKS, k_in))
                for j in ((0, 1) if q else (2, 3)):
                    split_steps.wait(sp, B, j, 3, still=still)
                    for i, part in enumerate(blocks):
                        row = DH * i + 8 * (j % 2)
                        sp.dma_start(dram[B.one(), row:row + 8].rearrange("a r h t -> (a r h) t"),
                                     parts[:, j, part, :]).then_inc(parts_out.sem, 16)
                parts_out.wait(sp, B, 1 if q else 3, 5, still=still)
                if B.n >= 2 or B.turn is not None:
                    st_full.wait(sp, B + (-2), H - 1, 1, still=still)
                    if q:
                        qx_done.wait(sp, B + (-2), still=still)
                rows = SHIFT if kind == SPLIT else PARTS
                sp.dma_start(tile[B.n % 2][0:rows, :, :],
                             dram[B.one(), 0:rows].rearrange("a r h t -> (a r) h t")).then_inc(here.sem, 16)

            def shift_dma(B, g):
                turn_free.wait(sp, B, "sh", g, still=still)
                sp.dma_start(q_stack[B.n % 2][SHIFT:SHIFT + 2, G * g:G * g + G, :],
                             shift_rows[:, :]).then_inc(shift_in.sem, 16)

            def load_residual(B):
                stored.wait(sp, B + (-1), still=still)
                sp.dma_start(x_res[:, :, :],
                             xs[B.s][B.one()].rearrange("a (t p) d -> p (a t) d", p=P)).then_inc(res_loaded.sem, 16)

            def store(B):
                res_done.wait(sp, B, 1, still=still)
                sp.dma_start(xs[B.s + 1][B.one()].rearrange("a (t p) d -> p (a t) d", p=P),
                             x_res[:, :, :]).then_inc(stored.sem, 16)

            def first(B):
                load_x(B)
                load_stack(B, True)
                load_stack(B, False)
                shift_dma(B, 0)

            def body(B):
                nxt = B.n + 1 < NB
                if nxt:
                    load_x(B + 1)
                if B.n:
                    load_residual(B + (-1))
                else:
                    sp.sem_inc(stored.sem, 16)
                shift_dma(B, 1)
                if nxt:
                    load_stack(B + 1, True)
                shift_dma(B, 2)
                if nxt:
                    load_stack(B + 1, False)
                shift_dma(B, 3)
                if B.n:
                    store(B + (-1))
                if nxt:
                    shift_dma(B + 1, 0)

            def finish(B):
                load_residual(B)
                store(B)

            n_class = 0
            for s, kind in enumerate(STAGES):
                if s:
                    stage_start(sp, s)
                if s == 1:
                    for dst, src in weights[ROTARY]:
                        sp.dma_start(dst, src).then_inc(rotary_in, 16)
                if kind == SPLIT:
                    base = NB * n_class
                    def class_batch(b, base=base):
                        wait_before(sp, c_xn, b, base, still)
                        sp.dma_start(x_new[:, :, :],
                                     xs[s][bass.ds(b, 1)].rearrange("a (t p) d -> p (a t) d", p=P)).then_inc(c_x, 16)

                    over_batches(sp, class_batch)
                    sp.wait_ge(c_rtc, n_class + 1)
                    sp.dma_start(mask_d.rearrange("k (b t) -> (k b) t", t=P).rearrange("(a c) t -> c a t", a=2),
                                 class_t[:, :, :]).then_inc(c_dram, 16)
                    sp.wait_ge(c_dram, 16 * (n_class + 1))
                    n = 0
                    for r in range(4):
                        dram = q_stack_d if r < 2 else k_stack_d
                        for h in range(H):
                            sp.dma_start(dram[:, MASK + r % 2, h, :],
                                         mask_d[r].rearrange("(b t) -> b t", b=NB)).then_inc(c_masks, 16)
                            n += 1
                    n_class += 1
                    sp.wait_ge(c_masks, 16 * n * n_class)
                run_stage(sp, s, first, body, finish)
            sp.wait_ge(stored.sem, 16 * (NB + 1) * len(STAGES))

        @block.gpsimd
        def _(pool):
            for i in range(2):
                nc.gpsimd.memset(values[i][:, :, :, DH:DH + 1], 1.0).then_inc(preset, 1)
                nc.gpsimd.memset(values[i][:, :, :, DH + 1:VW], 0.0).then_inc(preset, 1)
            nc.gpsimd.memset(minus_half[:, :], -0.5).then_inc(preset, 1)
            stage_start(pool, 0)

            def normalise(B):
                stats_done.wait(pool, B, still=still)
                nc.gpsimd.tensor_scalar(var_eps[:, :], mean_var[:, :, 1], EPS, None, ALU.add).then_inc(eps_done.sem, 1)
                eps_done.wait(pool, B, still=still)
                nc.gpsimd.tensor_tensor(rstd[:, :], var_eps[:, :], minus_half[:, 0:T], ALU.pow).then_inc(rstd_done.sem, 1)
                rstd_done.wait(pool, B, still=still)
                if B.n:
                    turn_full.wait(pool, B + (-1), "xt", 1, still=still)
                for t in range(T):
                    last = nc.gpsimd.tensor_scalar(xn[:, t, :], x_new[:, t, :], mean_var[:, t, 0:1],
                                                   rstd[:, t:t + 1], ALU.subtract, ALU.mult)
                last.then_inc(xn_done.sem, 1)

            def rotate(B, q):
                a, b = (0, 1) if q else (2, 3)
                turn_free.wait(pool, B, "qk", b, still=still)
                if q:
                    if B.n:
                        split_steps.wait(pool, B + (-1), 3, 3, still=still)
                else:
                    split_steps.wait(pool, B, 1, 3, still=still)
                for j, (own, other, op) in enumerate(((a, b, ALU.subtract), (b, a, ALU.add))):
                    if j:
                        rot_steps.wait(pool, B, a, 2, still=still)
                    nc.gpsimd.tensor_tensor(rot_a, qk_f[:, own, :], cos_t[:, :], ALU.mult).then_inc(rot_steps.sem, 1)
                    nc.gpsimd.tensor_tensor(rot_b, qk_f[:, other, :], sin_t[:, :], ALU.mult).then_inc(rot_steps.sem, 1)
                    rot_steps.wait(pool, B, a + j, 1, still=still)
                    nc.gpsimd.tensor_tensor(rot_f[:, j, :], rot_a, rot_b, op).then_inc(rot_steps.sem, 1)

            def split(B, j, src):
                if B.n:
                    parts_out.wait(pool, B + (-1), j, 5, still=still)
                nc.gpsimd.tensor_copy(parts[:, j, 0, :], src).then_inc(split_steps.sem, 1)
                split_steps.wait(pool, B, j, 0, still=still)
                nc.gpsimd.tensor_tensor(rest[:, :], src, parts[:, j, 0, :], ALU.subtract).then_inc(split_steps.sem, 1)
                split_steps.wait(pool, B, j, 1, still=still)
                nc.gpsimd.tensor_copy(parts[:, j, 1, :], rest[:, :]).then_inc(split_steps.sem, 1)
                split_steps.wait(pool, B, j, 2, still=still)
                nc.gpsimd.tensor_tensor(parts[:, j, 2, :], rest[:, :], parts[:, j, 1, :], ALU.subtract).then_inc(split_steps.sem, 1)

            def splits(B, q):
                rotary = STAGES[B.s] == ROTARY
                if rotary:
                    rotate(B, q)
                for m in range(2):
                    j = m + (0 if q else 2)
                    if rotary:
                        rot_steps.wait(pool, B, j, 2, still=still)
                        split(B, j, rot_f[:, m, :])
                    else:
                        turn_free.wait(pool, B, "qk", j, still=still)
                        split(B, j, qk_f[:, j, :])
                        pool.sem_inc(rot_steps.sem, 3)

            def bias_residual(B):
                res_loaded.wait(pool, B, still=still)
                kind = STAGES[B.s]
                if kind == ROTARY:
                    pool.sem_inc(res_biased.sem, 1)
                else:
                    nc.gpsimd.tensor_tensor(x_res[:, :, :], x_res[:, :, :],
                                            o_bias[kind][:, :].unsqueeze(1).broadcast_to([P, T, D]),
                                            ALU.add).then_inc(res_biased.sem, 1)

            def first(B):
                normalise(B)
                splits(B, True)
                splits(B, False)

            def body(B):
                nxt = B.n + 1 < NB
                if nxt:
                    normalise(B + 1)
                if B.n:
                    bias_residual(B + (-1))
                if nxt:
                    splits(B + 1, True)
                    splits(B + 1, False)

            n_class = 0
            for s, kind in enumerate(STAGES):
                if s:
                    stage_start(pool, s)
                if kind == SPLIT:
                    base = NB * n_class
                    if n_class == 0:
                        pool.wait_ge(g_step, 2)
                        nc.gpsimd.tensor_tensor(norms[:, 0:H], norms[:, H:2 * H], minus_half[:, 0:H], ALU.pow).then_inc(g_step, 1)
                    def class_batch(b, base=base):
                        wait_reg(pool, c_stats, b + (base + 1), still)
                        nc.gpsimd.tensor_scalar(var_eps[:, :], mean_var[:, :, 1], EPS, None, ALU.add).then_inc(c_eps, 1)
                        wait_reg(pool, c_eps, b + (base + 1), still)
                        nc.gpsimd.tensor_tensor(rstd[:, :], var_eps[:, :], minus_half[:, 0:T], ALU.pow).then_inc(c_rstd, 1)
                        wait_reg(pool, c_rstd, b + (base + 1), still)
                        wait_before(pool, c_tr, b, base, still)
                        for t in range(T):
                            last = nc.gpsimd.tensor_scalar(xn[:, t, :], x_new[:, t, :], mean_var[:, t, 0:1],
                                                           rstd[:, t:t + 1], ALU.subtract, ALU.mult)
                        last.then_inc(c_xn, 1)
                        wait_reg(pool, c_norm, b + (base + 1), still)
                        nc.gpsimd.tensor_tensor(cosines[:, :], norms[:, :], minus_half[:, :], ALU.pow).then_inc(c_inv, 1)

                    over_batches(pool, class_batch)
                    pool.wait_ge(c_ext, n_class + 1)
                    nc.gpsimd.partition_all_reduce(all_extremes[:, :], extremes[:, :], P, bass.bass_isa.ReduceOp.max).then_inc(c_all, 1)
                    n_class += 1
                run_stage(pool, s, first, body,
                          lambda B: bias_residual(B))

        @block.vector
        def _(dve):
            for i in range(2):
                nc.vector.memset(q_stack[i][PARTS:ROWS, :, :], 0.0).then_inc(preset, 1)
                nc.vector.memset(k_stack[i][PARTS:ROWS, :, :], 1.0).then_inc(preset, 1)
                nc.vector.memset(qx[i][0:QX_ROWS, :, :], 0.0).then_inc(preset, 1)
            nc.vector.memset(sm[0][:, :], 0.0).then_inc(preset, 1)
            nc.vector.memset(sm[1][:, :], 0.0).then_inc(preset, 1)
            stage_start(dve, 0)

            def statistics(B):
                x_loaded.wait(dve, B)
                for t in range(T):
                    last = nc.vector.bn_stats(bn[:, t, :], x_new[:, t, :])
                last.then_inc(bn_done.sem, 1)
                if B.n:
                    xn_done.wait(dve, B + (-1))
                bn_done.wait(dve, B, still=still)
                for t in range(T):
                    last = nc.vector.bn_aggr(mean_var[:, t, :], bn[:, t, :])
                last.then_inc(stats_done.sem, 1)

            def register_queries(B):
                if STAGES[B.s] == SPLIT:
                    q_in.wait(dve, B)
                    if B.n >= 2 or B.turn is not None:
                        sm_full.wait(dve, B + (-2), "extra", NG - 1)
                    nc.vector.tensor_copy(qx[B.n % 2][0:PARTS, :, 0:8],
                                          q_stack[B.n % 2][0:PARTS, :, 0:8]).then_inc(qx_done.sem, 1)
                else:
                    dve.sem_inc(qx_done.sem, 1)

            def maximum(B, h, t):
                kind = STAGES[B.s]
                if h % G == 0 and t == 0 and (h or B.n):
                    shift_ready.wait(dve, B + (0 if h else -1), (h // G - 1) % NG)
                sm_full.wait(dve, B, h, t)
                n = (t + 1) * P if kind == CAUSAL else L
                bank = sm[sm_full.position(B, h, t) % 2]
                nc.vector.tensor_reduce(neg_max[:, h % G, t:t + 1], bank[:, 0:n], AX.X, ALU.max,
                                        negate=True).then_inc(max_done.sem, 1)

            def shift(B, g):
                max_done.wait(dve, B, G * g + G - 1, T - 1)
                if g or B.n:
                    turn_full.wait(dve, B + (0 if g else -1), "sh", (g - 1) % NG)
                nm = neg_max[:, :, :].rearrange("p h t -> p (h t)")
                nc.vector.tensor_copy(shift_parts[:, 0, :], nm).then_inc(shift_high.sem, 1)
                shift_high.wait(dve, B, g)
                nc.vector.tensor_tensor(shift_parts[:, 1, :], nm, shift_parts[:, 0, :],
                                        ALU.subtract).then_inc(shift_ready.sem, 1)

            def extra_max(B, g):
                sm_full.wait(dve, B, "extra", g)
                if g or B.n:
                    xmax_exp.wait(dve, B + (0 if g else -1), (g - 1) % NG)
                bank = sm[sm_full.position(B, "extra", g) % 2]
                nc.vector.tensor_reduce(x_neg_max[:, :], bank[:, :], AX.X, ALU.max, negate=True).then_inc(max_done.sem, 1)

            def scale_output(B, g):
                turn_full.wait(dve, B, "og", g)
                if g or B.n:
                    o_scaled.wait(dve, B + (0 if g else -1), (g - 1) % NG)
                nc.vector.reciprocal(inv_sum[:, :], turn_heads[:, :, DH]).then_inc(o_inv.sem, 1)
                if B.n >= 2 or B.turn is not None:
                    turn_full.wait(dve, B + (-2), "ot", 1)
                o_inv.wait(dve, B, g)
                nc.vector.tensor_tensor(
                    att[B.n % 2][:, :, G * DH * g:G * DH * (g + 1)].rearrange("p t (h c) -> p t h c", h=G),
                    turn_heads[:, :, 0:DH].rearrange("p (t h) c -> p t h c", t=T),
                    inv_sum[:, :].rearrange("p (t h) -> p t h", t=T).unsqueeze(3).broadcast_to([P, T, G, DH]),
                    ALU.mult).then_inc(turn_free.sem, 1)
                turn_free.wait(dve, B, "og", g)
                dve.sem_inc(o_scaled.sem, 1)

            def mean_of_classes(B, g):
                turn_full.wait(dve, B, "xo", g)
                nc.vector.reciprocal(x_inv[0:REG, :], turn_heads[0:REG, 0:G, DH]).then_inc(extra_steps.sem, 1)
                extra_steps.wait(dve, B, g, 0)
                nc.vector.tensor_scalar(x_half[0:REG, :], x_inv[0:REG, :], 0.5, None, ALU.mult).then_inc(extra_steps.sem, 1)
                extra_steps.wait(dve, B, g, 1)
                nc.vector.tensor_tensor(x_out[0:REG, :, :], turn_heads[0:REG, 0:G, 0:DH],
                                        x_half[0:REG, :].unsqueeze(2).broadcast_to([REG, G, DH]), ALU.mult).then_inc(extra_steps.sem, 1)
                extra_steps.wait(dve, B, g, 2)
                reg = att[B.n % 2][0:REG, 0, G * DH * g:G * DH * (g + 1)]
                nc.vector.scalar_tensor_tensor(out=reg, in0=reg, scalar=0.5,
                                               in1=x_out[0:REG, :, :].rearrange("p h c -> p (h c)"),
                                               op0=ALU.mult, op1=ALU.add).then_inc(turn_free.sem, 1)
                turn_free.wait(dve, B, "xo", g)
                dve.sem_inc(extra_steps.sem, 1)

            def take_turn(B, k, i):
                kind = STAGES[B.s]
                if B.turn is None and B.n < 0:
                    turn_full.wait_earlier(dve, B, 0, k, i)
                    dve.sem_inc(turn_free.sem, 1)
                elif k == "v" and kind == CAUSAL:
                    turn_full.wait(dve, B, k, i)
                    if B.n >= 2 or B.turn is not None:
                        pv_done.wait(dve, B + (-2), NG - 1, T - 1)
                    for t in range(2):
                        last = nc.vector.tensor_tensor(
                            values[B.n % 2][:, 2 * i + t, :, 0:DH],
                            turn_ps[:, D * t:D * (t + 1)].rearrange("p (h c) -> p h c", h=H),
                            v_bias[:, :].rearrange("p (h c) -> p h c", h=H), ALU.add)
                    last.then_inc(turn_free.sem, 1)
                elif k == "sh":
                    turn_full.wait(dve, B, k, i)
                    if i or B.n:
                        shift_in.wait(dve, B + (0 if i else -1), (i - 1) % NG)
                    nc.vector.tensor_copy(shift_rows[:, :], turn_b[0:2 * G * T, :]).then_inc(turn_free.sem, 1)
                elif k == "og":
                    scale_output(B, i)
                elif k == "xo":
                    mean_of_classes(B, i)
                elif k == "out":
                    turn_full.wait(dve, B, k, i)
                    res_biased.wait(dve, B)
                    half = x_res[:, 2 * i:2 * i + 2, :].rearrange("p t d -> p (t d)")
                    nc.vector.tensor_tensor(half, turn_ps[:, :], half, ALU.add).then_inc(turn_free.sem, 1)
                    dve.wait_ge(turn_free.sem, turn_free.after(B, k, i))
                    dve.sem_inc(res_done.sem, 1)

            def first(B):
                statistics(B)
                if STAGES[B.s] == CAUSAL:
                    take_turn(B, "v", 0)
                    take_turn(B, "v", 1)
                for h in range(AHEAD):
                    for t in range(T):
                        maximum(B, h, t)
                    if h == G - 1:
                        shift(B, 0)
                take_turn(B, "sh", 0)
                register_queries(B)

            def body(B):
                kind = STAGES[B.s]
                if B.n + 1 < NB:
                    statistics(B + 1)
                for slot in range(H):
                    m = max_head(B.n, slot)
                    for place in range(2):
                        if m:
                            maximum(B + m[0], m[1], 2 * place)
                            maximum(B + m[0], m[1], 2 * place + 1)
                        if place == 0:
                            for k, off, i in turns_of(kind, B.n, slot, 0):
                                take_turn(B + off, k, i)
                    if kind == SPLIT and slot % G == 1:
                        extra_max(B, slot // G)
                    if m and m[1] % G == G - 1:
                        shift(B + m[0], m[1] // G)
                    for k, off, i in turns_of(kind, B.n, slot, 1):
                        take_turn(B + off, k, i)
                if B.n + 1 < NB:
                    register_queries(B + 1)

            def finish(B):
                for k, i in finish_turns(STAGES[B.s]):
                    take_turn(B, k, i)

            n_class = 0
            n_clear = 0
            for s, kind in enumerate(STAGES):
                if s:
                    stage_start(dve, s)
                if kind == ROTARY:
                    for i in range(2):
                        nc.vector.memset(q_stack[i][MASK:MASK + 2, :, :], 0.0).then_inc(masks_cleared, 1)
                if kind == SPLIT:
                    base = NB * n_class
                    if n_class == 0:
                        nc.vector.tensor_tensor(prod[:, 0, :], guide[:, :], guide[:, :], ALU.mult).then_inc(g_step, 1)
                        dve.wait_ge(g_step, 1)
                        nc.vector.tensor_reduce(norms[:, H:2 * H], prod[:, 0, :].rearrange("p (h c) -> p h c", h=H),
                                                AX.X, ALU.add).then_inc(g_step, 1)
                        dve.wait_ge(g_step, 3)
                        nc.vector.tensor_tensor(guide[:, :].rearrange("p (h c) -> p h c", h=H),
                                                guide[:, :].rearrange("p (h c) -> p h c", h=H),
                                                norms[:, 0:H].unsqueeze(2).broadcast_to([P, H, DH]), ALU.mult).then_inc(g_step, 1)
                        dve.wait_ge(g_step, 4)
                    def class_batch(b, base=base):
                        dve.wait_ge(c_x, b * 16 + 16 * (base + 1))
                        for t in range(T):
                            last = nc.vector.bn_stats(bn[:, t, :], x_new[:, t, :])
                        last.then_inc(c_bn, 1)
                        wait_before(dve, c_xn, b, base)
                        wait_reg(dve, c_bn, b + (base + 1), still)
                        for t in range(T):
                            last = nc.vector.bn_aggr(mean_var[:, t, :], bn[:, t, :])
                        last.then_inc(c_stats, 1)
                        dve.wait_ge(c_q, b + (base + 1))
                        for t in range(T):
                            last = nc.vector.tensor_tensor(prod[:, t, :], st[0][:, D * t:D * (t + 1)], guide[:, :], ALU.mult)
                        last.then_inc(c_prod, 1)
                        dve.wait_ge(c_prod, b + (base + 1))
                        nc.vector.tensor_reduce(dots[:, :], prod.rearrange("p t (h c) -> p (t h) c", h=H),
                                                AX.X, ALU.add).then_inc(c_dots, 1)
                        dve.wait_ge(c_sq, b + (base + 1))
                        nc.vector.tensor_reduce(norms[:, :], square.rearrange("p t (h c) -> p (t h) c", h=H),
                                                AX.X, ALU.add).then_inc(c_norm, 1)
                        dve.wait_ge(c_inv, b + (base + 1))
                        nc.vector.tensor_tensor(dots[:, :], dots[:, :], cosines[:, :], ALU.mult).then_inc(c_cos, 1)
                        dve.wait_ge(c_cos, b + (base + 1))
                        nc.vector.tensor_reduce(sim_b[:, :], dots[:, :].rearrange("p (t h) -> p t h", h=H),
                                                AX.X, ALU.add).then_inc(c_simb, 1)
                        dve.wait_ge(c_simb, b + (base + 1))
                        nc.vector.tensor_scalar(sim[:, bass.ds(b * T, T)], sim_b[:, :], 1.0 / H, None, ALU.mult).then_inc(c_sim, 1)

                    over_batches(dve, class_batch)
                    steps = [0]

                    def link(ins):
                        steps[0] += 1
                        ins.then_inc(c_step, 1)
                        dve.wait_ge(c_step, STEPS * n_class + steps[0])

                    STEPS = 15
                    dve.wait_ge(c_sim, NB * (n_class + 1))
                    link(nc.vector.tensor_tensor(cls[:, 0, :], sim[:, :], reg_big[:, :], ALU.add))
                    link(nc.vector.tensor_reduce(spread[:, 0:1], cls[:, 0, :], AX.X, ALU.min))
                    link(nc.vector.tensor_tensor(cls[:, 1, :], sim[:, :], reg_big[:, :], ALU.subtract))
                    link(nc.vector.tensor_scalar(extremes[:, 0:1], spread[:, 0:1], -1.0, None, ALU.mult))
                    nc.vector.tensor_reduce(extremes[:, 1:2], cls[:, 1, :], AX.X, ALU.max).then_inc(c_ext, 1)
                    dve.wait_ge(c_all, n_class + 1)
                    link(nc.vector.tensor_tensor(spread[:, 0:1], all_extremes[:, 1:2], all_extremes[:, 0:1], ALU.add))
                    link(nc.vector.reciprocal(spread[:, 1:2], spread[:, 0:1]))
                    link(nc.vector.tensor_scalar(cls[:, 0, :], sim[:, :], all_extremes[:, 0:1], spread[:, 1:2],
                                                 ALU.add, ALU.mult))
                    link(nc.vector.tensor_scalar(cls[:, 1, :], cls[:, 0, :], 0.9, None, ALU.is_gt))
                    link(nc.vector.tensor_scalar(cls[:, 2, :], reg_big[:, :], 0.0, None, ALU.is_gt))
                    link(nc.vector.tensor_tensor(cls[:, 0, :], cls[:, 1, :], cls[:, 2, :], ALU.max))
                    link(nc.vector.tensor_copy(class_rows[:, 0, :], cls[:, 0, :]))
                    link(nc.vector.tensor_scalar(class_rows[:, 1, :], cls[:, 0, :], -1.0, 1.0, ALU.mult, ALU.add))
                    link(nc.vector.tensor_scalar(class_rows[:, 2, :], cls[:, 0, :], BIG, -BIG, ALU.mult, ALU.add))
                    link(nc.vector.tensor_tensor(cls[:, 0, :], cls[:, 0, :], cls[:, 2, :], ALU.subtract))
                    link(nc.vector.tensor_scalar(class_rows[:, 3, :], cls[:, 0, :], -BIG, None, ALU.mult))
                    assert steps[0] == STEPS
                    dve.sem_inc(c_rows, 1)
                    dve.wait_ge(c_rt, n_class + 1)
                    nc.vector.tensor_copy(class_t[:, 0, :], turn_b)
                    nc.vector.tensor_copy(class_t[:, 1, :], turn_b2).then_inc(c_rtc, 1)
                    n_class += 1
                run_stage(dve, s, first, body, finish)

        @block.scalar
        def _(act):
            stage_start(act, 0)
            nc.scalar.mul(q_bias[:, :], qk_bias[:, 0:KT], DH ** -0.5).then_inc(masks_cleared, 1)

            def exponential(B, h, c, i):
                kind = STAGES[B.s]
                st_full.wait(act, B, h, c)
                g = h // G
                if h % G == 0 and (g or B.n):
                    pv_done.wait(act, B + (0 if g else -1), (g - 1) % NG, 2 * c + 1)
                n = chunk_offset(kind, 2 * c + 1) + L - key_start(kind, 2 * c + 1)
                nc.scalar.activation(probs[c][:, h % G, 0:n], st[i][:, 0:n], ACT.Exp).then_inc(exp_done.sem, 1)

            def take_sums(B, g):
                pv_done.wait(act, B, g, T - 1)
                if g or B.n:
                    turn_full.wait(act, B + (0 if g else -1), "og", (g - 1) % NG)
                nc.scalar.copy(out_sums[:, :], o_ps[:, :]).then_inc(o_taken.sem, 1)

            def extra_exp(B, g):
                max_done.wait(act, B, "extra", g)
                if g or B.n:
                    turn_full.wait(act, B + (0 if g else -1), "ex", (g - 1) % NG)
                bank = sm[sm_full.position(B, "extra", g) % 2]
                nc.scalar.activation(x_probs[:, :], bank[:, :], ACT.Exp, bias=x_neg_max[:, :]).then_inc(xmax_exp.sem, 1)

            def take_turn(B, k, i):
                kind = STAGES[B.s]
                if B.turn is None and B.n < 0:
                    return
                if k == "xt":
                    turn_full.wait(act, B, k, i)
                    nc.scalar.copy(xn_t[:, i, :], turn_ps[:, :]).then_inc(turn_free.sem, 1)
                elif k == "qk":
                    turn_full.wait(act, B, k, i)
                    if B.n:
                        split_steps.wait(act, B + (-1), 3 if i > 1 else 1, 3)
                    scale = DH ** -0.5 if i < 2 else 1.0
                    if kind == CAUSAL:
                        bias = q_bias[:, i:i + 1] if i < 2 else qk_bias[:, i:i + 1]
                        nc.scalar.activation(qk_f[:, i, :], turn_ps[:, :], ACT.Identity, bias=bias,
                                             scale=scale).then_inc(turn_free.sem, 1)
                    else:
                        nc.scalar.activation(qk_f[:, i, :], turn_ps[:, :], ACT.Copy, scale=scale).then_inc(turn_free.sem, 1)
                elif k == "v" and kind != CAUSAL:
                    turn_full.wait(act, B, k, i)
                    if B.n >= 2 or B.turn is not None:
                        pv_done.wait(act, B + (-2), NG - 1, T - 1)
                    for t in range(2):
                        last = nc.scalar.copy(values[B.n % 2][:, 2 * i + t, :, 0:DH],
                                              turn_ps[:, D * t:D * (t + 1)].rearrange("p (h c) -> p h c", h=H))
                    last.then_inc(turn_free.sem, 1)
                elif k == "ot":
                    turn_full.wait(act, B, k, i)
                    nc.scalar.copy(att_t[:, i, :], turn_ps[:, :]).then_inc(turn_free.sem, 1)
                elif k == "ex":
                    turn_full.wait(act, B, k, i)
                    if i or B.n:
                        turn_full.wait(act, B + (0 if i else -1), "xo", (i - 1) % NG)
                    nc.scalar.copy(x_probs_t[:, :, :].rearrange("p t c -> p (t c)"), turn_ps[:, :]).then_inc(turn_free.sem, 1)

            def first(B):
                if B.s == 0:
                    act.wait_ge(masks_cleared, 1)
                for k, i in PREPARE:
                    take_turn(B, k, i)

            def body(B):
                kind = STAGES[B.s]
                for slot in range(H):
                    if kind == SPLIT and slot % G == 2:
                        extra_exp(B, slot // G)
                    off, g, kt = values_of(slot)
                    for place, (h, c) in enumerate(chunks_of(slot)):
                        exponential(B, h, c, place)
                        if place and kt == T - 1 and B.n + off >= 0:
                            take_sums(B + off, g)
                        for k, o, i in turns_of(kind, B.n, slot, place):
                            take_turn(B + o, k, i)

            def finish(B):
                take_sums(B, NG - 1)
                for k, i in finish_turns(STAGES[B.s]):
                    take_turn(B, k, i)

            n_class = 0
            for s, kind in enumerate(STAGES):
                if s:
                    stage_start(act, s)
                if kind == SPLIT:
                    base = NB * n_class
                    def class_batch(b, base=base):
                        act.wait_ge(c_tr, b + (base + 1))
                        nc.scalar.copy(xn_t[:, :, :].rearrange("p k t -> p (k t)"), st[1][:, :]).then_inc(c_trc, 1)
                        act.wait_ge(c_prod, b + (base + 1))
                        wait_before(act, c_norm, b, base)
                        nc.scalar.activation(square.rearrange("p t d -> p (t d)"), st[0][:, :], ACT.Square).then_inc(c_sq, 1)

                    over_batches(act, class_batch)
                    n_class += 1
                run_stage(act, s, first, body, finish)

        @block.tensor
        def _(pe):
            stage_start(pe, 0)

            def score_rows(kind, shifted):
                return ROWS if shifted else (SHIFT if kind == SPLIT else PARTS)

            def max_tiles(B, h, tiles, slot_in_group):
                kind = STAGES[B.s]
                if h == 0 and 0 in tiles:
                    q_in.wait(pe, B)
                    k_in.wait(pe, B)
                r = score_rows(kind, False)
                q, k = q_stack[B.n % 2], k_stack[B.n % 2]
                for t in tiles:
                    max_done.wait_earlier(pe, B, 2, h, t)
                    if t == 1 and slot_in_group is not None:
                        xmax_exp.wait(pe, *slot_in_group)
                    n = (t + 1) * P if kind == CAUSAL else L
                    bank = sm[sm_full.position(B, h, t) % 2]
                    last = nc.tensor.matmul(bank[:, 0:n], q[0:r, h, t * P:(t + 1) * P], k[0:r, h, 0:n],
                                            start=True, stop=kind != CAUSAL)
                    if kind == CAUSAL:
                        last = nc.tensor.matmul(bank[:, t * P:(t + 1) * P], ident_b[:, :], causal_qk[:, :],
                                                start=False, stop=True)
                    last.then_inc(sm_full.sem, 1)

            def extra_tile(B, g):
                qx_done.wait(pe, B)
                max_done.wait_earlier(pe, B, 2, "extra", g)
                bank = sm[sm_full.position(B, "extra", g) % 2]
                for i in range(G):
                    h = G * g + i
                    last = nc.tensor.matmul(bank[XW * i:XW * (i + 1), :], qx[B.n % 2][0:SHIFT, h, :],
                                            k_stack[B.n % 2][0:SHIFT, h, :], start=True, stop=True)
                last.then_inc(sm_full.sem, 1)

            def scores_t(B, h, c, i):
                kind = STAGES[B.s]
                if h % G == 0 and c == 0:
                    shift_in.wait(pe, B, h // G)
                if kind == ROTARY and B.n == 0 and h == 0:
                    pe.wait_ge(masks_cleared, 3)
                q, k = q_stack[B.n % 2], k_stack[B.n % 2]
                exp_done.wait_earlier(pe, B, 2, h, c)
                for kt in (2 * c, 2 * c + 1):
                    q0 = key_start(kind, kt)
                    off = chunk_offset(kind, kt)
                    last = nc.tensor.matmul(st[i][:, off:off + L - q0], k[0:ROWS, h, kt * P:(kt + 1) * P],
                                            q[0:ROWS, h, q0:L], start=True, stop=kind != CAUSAL)
                    if kind == CAUSAL:
                        last = nc.tensor.matmul(st[i][:, off:off + P], ident_b[:, :], causal_kq[:, :],
                                                start=False, stop=True)
                last.then_inc(st_full.sem, 1)

            def output_sums(B, g, kt):
                kind = STAGES[B.s]
                exp_done.wait(pe, B, G * g + G - 1, kt // 2)
                if g == 0 and kt == 0:
                    turn_free.wait(pe, B, "v", 1)
                if kt == 0 and (g or B.n):
                    o_taken.wait(pe, B + (0 if g else -1), (g - 1) % NG)
                q0, off = key_start(kind, kt), chunk_offset(kind, kt)
                for h in range(G):
                    last = nc.tensor.matmul(o_ps[VW * h:VW * (h + 1), q0:L], values[B.n % 2][:, kt, G * g + h, :],
                                            probs[kt // 2][:, h, off:off + L - q0], start=kt == 0, stop=kt == T - 1)
                last.then_inc(pv_done.sem, 1)

            def turn(B, k, i):
                kind = STAGES[B.s]
                if B.turn is None and B.n < 0:
                    turn_free.wait_earlier(pe, B, 1, k, i)
                    pe.sem_inc(turn_full.sem, 1)
                    return
                if k == "xt":
                    xn_done.wait(pe, B)
                elif k == "sh":
                    shift_ready.wait(pe, B, i)
                elif k == "ex":
                    xmax_exp.wait(pe, B, i)
                elif k == "og":
                    o_taken.wait(pe, B, i)
                turn_free.wait_earlier(pe, B, 1, k, i)
                if k == "xt":
                    for t in range(T):
                        last = nc.tensor.transpose(turn_ps[:, t * P:(t + 1) * P], xn[:, t, i * P:(i + 1) * P], ident[:, :])
                elif k == "qk":
                    weight = (wq if i < 2 else wk)[kind]
                    m = i % 2
                    for kt in range(KT):
                        last = nc.tensor.matmul(turn_ps[:, :], weight[:, kt, m * P:(m + 1) * P], xn_t[:, kt, :],
                                                start=kt == 0, stop=kt == KT - 1)
                elif k == "v":
                    for j in range(2):
                        t = 2 * i + j
                        for kt in range(KT):
                            last = nc.tensor.matmul(turn_ps[:, j * D:(j + 1) * D], xn_t[:, kt, t * P:(t + 1) * P],
                                                    wv[kind][:, kt, :], start=kt == 0, stop=kt == KT - 1)
                elif k == "sh":
                    last = nc.tensor.transpose(turn_b[0:2 * G * T, :],
                                               shift_parts[:, :, :].rearrange("p a c -> p (a c)"), ident_b[:, :])
                elif k == "ex":
                    for t in range(T):
                        last = nc.tensor.transpose(turn_ps[:, t * P:(t + 1) * P], x_probs[:, t * P:(t + 1) * P], ident[:, :])
                elif k == "og":
                    for t in range(T):
                        last = nc.tensor.transpose(turn_ps[:, t * P:(t + 1) * P], out_sums[:, t * P:(t + 1) * P], ident[:, :])
                elif k == "xo":
                    for h in range(G):
                        for kt in range(T):
                            last = nc.tensor.matmul(turn_heads[0:8, h, :], x_probs_t[:, kt, XW * h:XW * h + 8],
                                                    values[B.n % 2][:, kt, G * i + h, :], start=kt == 0, stop=kt == T - 1)
                elif k == "ot":
                    for t in range(T):
                        last = nc.tensor.transpose(turn_ps[:, t * P:(t + 1) * P], att[B.n % 2][:, t, i * P:(i + 1) * P], ident[:, :])
                elif k == "out":
                    for j in range(2):
                        t = 2 * i + j
                        for kt in range(KT):
                            last = nc.tensor.matmul(turn_ps[:, j * D:(j + 1) * D], att_t[:, kt, t * P:(t + 1) * P],
                                                    wo[kind][:, kt, :], start=kt == 0, stop=kt == KT - 1)
                last.then_inc(turn_full.sem, 1)

            def first(B):
                for k, i in PREPARE:
                    turn(B, k, i)
                for h in range(AHEAD):
                    max_tiles(B, h, range(T), None)
                turn(B, "sh", 0)

            def body(B):
                kind = STAGES[B.s]
                for slot in range(H):
                    m = max_head(B.n, slot)
                    after_extra = (B, slot // G) if kind == SPLIT and slot % G == 2 else None

                    def max_tile(t):
                        if m:
                            max_tiles(B + m[0], m[1], [t], after_extra)

                    def turns(place):
                        for k, off, i in turns_of(kind, B.n, slot, place):
                            turn(B + off, k, i)

                    (h0, c), (h1, _) = chunks_of(slot)
                    off, g, kt = values_of(slot)
                    scores_t(B, h0, c, 0)
                    max_tile(0)
                    turns(0)
                    max_tile(1)
                    scores_t(B, h1, c, 1)
                    max_tile(2)
                    if B.n + off >= 0:
                        output_sums(B + off, g, kt)
                    turns(1)
                    max_tile(3)
                    if kind == SPLIT and slot % G == 1:
                        extra_tile(B, slot // G)

            def finish(B):
                output_sums(B, NG - 1, T - 2)
                output_sums(B, NG - 1, T - 1)
                for k, i in finish_turns(STAGES[B.s]):
                    turn(B, k, i)

            n_class = 0
            for s, kind in enumerate(STAGES):
                if s:
                    stage_start(pe, s)
                if kind == ROTARY:
                    pe.wait_ge(rotary_in, 16 * len(weights[ROTARY]))
                if kind == SPLIT:
                    base = NB * n_class
                    def class_batch(b, base=base):
                        pe.wait_ge(c_xn, b + (base + 1))
                        wait_before(pe, c_trc, b, base)
                        for kt in range(KT):
                            for t in range(T):
                                last = nc.tensor.transpose(st[1][:, kt * L + t * P:kt * L + (t + 1) * P],
                                                           xn[:, t, kt * P:(kt + 1) * P], ident[:, :])
                        last.then_inc(c_tr, 1)
                        pe.wait_ge(c_trc, b + (base + 1))
                        wait_before(pe, c_prod, b, base)
                        wait_before(pe, c_sq, b, base)
                        for t in range(T):
                            for kt in range(KT):
                                last = nc.tensor.matmul(st[0][:, D * t:D * (t + 1)], xn_t[:, kt, t * P:(t + 1) * P],
                                                        wq_class[:, kt, :], start=kt == 0, stop=kt == KT - 1)
                        last.then_inc(c_q, 1)

                    over_batches(pe, class_batch)
                    pe.wait_ge(c_rows, n_class + 1)
                    rows = class_rows[:, :, :].rearrange("p k c -> p (k c)")
                    nc.tensor.transpose(turn_b, rows[:, 0:P], ident_b[:, :])
                    nc.tensor.transpose(turn_b2, rows[:, P:2 * P], ident_b[:, :]).then_inc(c_rt, 1)
                    n_class += 1
                run_stage(pe, s, first, body, finish)


def kernel(**inputs):
    import ml_dtypes
    import numpy as np
    import concourse.bacc as bacc
    from concourse.bass_utils import run_bass_kernel_spmd

    a = {k: np.asarray(v) for k, v in inputs.items()}

    def by_feature(m):
        return m.reshape(D, H, DH).transpose(0, 2, 1).reshape(D, D)

    def columns(v):
        return v.reshape(H, DH).transpose(1, 0).reshape(KT, P).transpose(1, 0)

    def on_all(v):
        return np.broadcast_to(v.reshape(1, D), (P, D))

    w = {}
    for kind, q, k, v, o in (
        (CAUSAL, a["L0_attn_a_Wq"].T, a["L0_attn_a_Wk"].T, a["L0_attn_a_Wv"].T, a["L0_attn_a_Wo"].T),
        (SPLIT, *np.split(a["L0_ffn_W_qkv"], 3, axis=1), a["L0_ffn_W_proj"]),
        (ROTARY, *np.split(a["L0_attn_b_Wqkv"], 3, axis=1), a["L0_attn_b_Wo"]),
    ):
        w[f"wq_{kind}"], w[f"wk_{kind}"], w[f"wv_{kind}"], w[f"wo_{kind}"] = by_feature(q), by_feature(k), v, o
        if kind == SPLIT:
            w["wq_class"] = q
    w["qk_bias"] = np.concatenate([columns(a["L0_attn_a_bq"]), columns(a["L0_attn_a_bk"])], axis=1)
    w["v_bias"] = on_all(a["L0_attn_a_bv"])
    w["o_bias_causal"] = on_all(a["L0_attn_a_bo"])
    w["o_bias_split"] = on_all(a["L0_ffn_b_proj"])
    w["guide"] = on_all(a["L0_ffn_g_info"][0, 0])

    freq = (1.0 / np.float32(10000.0) ** (np.arange(0, DH, 2, dtype=np.float32) / np.float32(DH))).astype(np.float32)
    angle = np.outer(freq, np.arange(L, dtype=np.float32)).astype(np.float32)
    later = np.arange(P)[:, None] > np.arange(P)[None, :]
    c = {
        "cos": np.repeat(np.cos(angle), H, axis=0).astype(np.float32),
        "sin": np.repeat(np.sin(angle), H, axis=0).astype(np.float32),
        "ident": np.eye(P, dtype=np.float32),
        "ident_b": np.eye(P).astype(ml_dtypes.bfloat16),
        "causal_kq": np.where(later, -BIG, 0.0).astype(ml_dtypes.bfloat16),
        "causal_qk": np.where(later.T, -BIG, 0.0).astype(ml_dtypes.bfloat16),
        "reg_big": np.where((np.arange(P)[:, None] < REG) & (np.arange(NB * T)[None, :] % T == 0), 1e30, 0.0).astype(np.float32),
        "neg_class": np.repeat(np.array([[0.0], [1.0]]), H * XW, axis=1).astype(ml_dtypes.bfloat16),
    }

    nc = bacc.Bacc("TRN2", target_bir_lowering=False, num_devices=1)
    arrays = {}

    def put(name, value):
        value = np.ascontiguousarray(value)
        arrays[name] = value
        return nc.dram_tensor(name, value.shape, mybir.dt.from_np(value.dtype), kind="ExternalInput").ap()

    x_in = put("x", a["L0_attn_a_x"])
    w = {n: put("w_" + n, v) for n, v in w.items()}
    c = {n: put("c_" + n, v) for n, v in c.items()}
    out = nc.dram_tensor("out", (NB, L, D), F32, kind="ExternalOutput").ap()
    hybrid_blocks(nc, x_in, w, c, out)
    result = run_bass_kernel_spmd(nc, [arrays], core_ids=[0])
    return result.results[0]["out"]
```

```python
from contextlib import ExitStack

import concourse.bass as bass
from concourse import mybir

F32 = mybir.dt.float32
BF16 = mybir.dt.bfloat16
ALU = mybir.AluOpType
ACT = mybir.ActivationFunctionType
AX = mybir.AxisListType

P = 128
NB = 16
L = 512
D = 256
H = 16
DH = D // H
T = L // P
KT = D // P
G = 4
NG = H // G
REG = 5
XW = 32
EPS = 1e-5
PARTS = 6 * DH
MASK = PARTS
SHIFT = PARTS + 2
ROWS = PARTS + 4
VW = 32
AHEAD = 6
BIG = float(2.0 ** 100)

CAUSAL, SPLIT, ROTARY = "causal", "split", "rotary"
STAGES = [CAUSAL, SPLIT, ROTARY, SPLIT]

Q_BLOCKS = [0, 0, 0, 1, 1, 2]
K_BLOCKS = [0, 1, 2, 0, 1, 0]

TURNS = {
    1: ([("xt", 1, 0)], [("xt", 1, 1)]),
    2: ([("qk", 1, 2)], [("sh", 0, 1)]),
    3: ([("qk", 1, 3)], [("qk", 1, 0)]),
    4: ([("qk", 1, 1)], [("og", -1, 3)]),
    5: ([("xo", -1, 3)], [("ex", 0, 0)]),
    6: ([], [("sh", 0, 2)]),
    7: ([("og", 0, 0)], []),
    8: ([("xo", 0, 0)], [("v", 1, 0)]),
    9: ([("ex", 0, 1)], [("v", 1, 1)]),
    10: ([("ot", -1, 0)], [("sh", 0, 3)]),
    11: ([("og", 0, 1)], [("ot", -1, 1)]),
    12: ([("xo", 0, 1)], [("out", -1, 0)]),
    13: ([("ex", 0, 2)], [("out", -1, 1)]),
    14: ([("og", 0, 2)], [("sh", 1, 0)]),
    15: ([("xo", 0, 2)], [("ex", 0, 3)]),
}
PREPARE = [("xt", 0), ("xt", 1), ("qk", 2), ("qk", 3), ("qk", 0), ("qk", 1), ("v", 0), ("v", 1)]
NORMALISE_AT = (0, 1)
PREPARE_AT = [(3, 1), (4, 0), (4, 1), (5, 0), (5, 1), (6, 0), (6, 1)]
PREP_STEPS = len(PREPARE_AT)
STORE_AT = 14


def finish_turns(kind):
    return ([("og", 3)] + ([("xo", 3)] if kind == SPLIT else [])
            + [("ot", 0), ("ot", 1), ("out", 0), ("out", 1)])


def chunks_of(slot):
    g, c, pair = slot // G, slot % G // 2, slot % 2
    return [(G * g + 2 * pair + i, c) for i in range(2)]


def values_of(slot):
    n = slot - 2
    return (0, n // T, n % T) if n >= 0 else (-1, NG - 1, T + n)


def turns_of(kind, b, slot, place=None):
    first, second = TURNS.get(slot, ([], []))
    turns = first + second if place is None else (first, second)[place]
    return [t for t in turns if b + t[1] < NB and (t[0] not in ("ex", "xo") or kind == SPLIT)]


def max_head(b, slot):
    h = slot + AHEAD
    off, h = (0, h) if h < H else (1, h - H)
    return (off, h) if b + off < NB else None


def key_start(kind, kt):
    return kt * P if kind == CAUSAL else 0


def chunk_offset(kind, kt):
    return (L - key_start(kind, kt - 1)) if kt % 2 else 0


class Batch:

    def __init__(self, s, n, turn=None):
        self.s, self.n, self.turn = s, n, turn

    def __add__(self, k):
        return Batch(self.s, self.n + k, self.turn)

    def index(self):
        return self.n if self.turn is None else self.turn * 2 + self.n

    def one(self):
        return bass.ds(self.index(), 1)


LOOPS = (NB - 2) // 2


def over_batches(eng, body):
    body(0)
    with eng.Fori(1, NB, 1) as b:
        body(b)


def one_ahead(eng, ahead, work, after=lambda b: None):
    ahead(0)
    after(0)
    ahead(1)
    work(0)
    after(1)
    with eng.Fori(1, NB - 1, 1) as b:
        ahead(b + 1)
        work(b)
        after(b + 1)
    work(NB - 1)


def wait_before(eng, sem, b, base, still=None):
    if not isinstance(b, int) or b + base:
        wait_reg(eng, sem, b + base, still)


def wait_reg(eng, sem, value, still=None):
    eng.wait_ge(sem, value)
    if still is not None and not isinstance(value, int):
        eng.sem_inc(still, 1)


class Count:

    def __init__(self, sem, labels, step=1):
        self.sem, self.step = sem, step
        self.at = {lab: (i + 1) * step for i, lab in enumerate(labels)}
        assert len(self.at) == len(labels)

    def after(self, B, *label):
        lab = lambda n: (B.s, n) + label
        if B.turn is None:
            return self.at[lab(B.n)]
        second = self.at[lab(B.n + 2)]
        d = self.at[lab(B.n + 4)] - second
        c = second - d
        assert c > 0 and all(self.at.get(lab(B.n + 2 * i), c) == c + d * i for i in range(LOOPS))
        return B.turn * d + c

    def wait(self, eng, B, *label, still=None):
        if B.turn is None and B.n < 0:
            return
        wait_reg(eng, self.sem, self.after(B, *label), still)

    def wait_earlier(self, eng, B, back, *label):
        v = self.after(B, *label) - self.step * back
        if B.turn is None and v <= 0:
            return
        eng.wait_ge(self.sem, v)

    def position(self, B, *label):
        return self.at[(B.s, B.n) + label] // self.step - 1


def steps_of(per_body, first=None, last=None):
    out = []
    for s, kind in enumerate(STAGES):
        if first:
            out += [(s, 0) + lab for lab in first(kind)]
        for b in range(NB):
            out += [(s, b + off) + lab for off, lab in per_body(kind, b)]
        if last:
            out += [(s, NB - 1) + lab for lab in last(kind)]
    return out


def hybrid_blocks(nc, x_in, w, consts, out):
    ctx = ExitStack()
    with ctx:
        def sb(name, shape, dt=F32):
            return ctx.enter_context(nc.sbuf_tensor(name, shape, dt))

        def ps(name, shape):
            return ctx.enter_context(nc.psum_tensor(name, shape, F32))

        def sem(name):
            return ctx.enter_context(nc.semaphore(name))

        xs = [x_in] + [nc.dram_tensor(f"x_after_{s}", (NB, L, D), F32, kind="Internal").ap() for s in range(3)] + [out]
        mask_d = nc.dram_tensor("mask_d", (4, NB * L), BF16, kind="Internal").ap()

        wq = {k: sb(f"wq_{k}", [P, KT, D]) for k in (CAUSAL, SPLIT)}
        wk = {k: sb(f"wk_{k}", [P, KT, D]) for k in (CAUSAL, SPLIT)}
        wv = {k: sb(f"wv_{k}", [P, KT, D]) for k in (CAUSAL, SPLIT)}
        wo = {k: sb(f"wo_{k}", [P, KT, D]) for k in (CAUSAL, SPLIT)}
        for tile in (wq, wk, wv, wo):
            tile[ROTARY] = tile[CAUSAL]
        wq_class = sb("wq_class", [P, KT, D])
        qk_bias = sb("qk_bias", [P, 2 * KT])
        q_bias = sb("q_bias", [P, KT])
        v_bias = sb("v_bias", [P, D])
        o_bias = {CAUSAL: sb("o_bias_c", [P, D]), SPLIT: sb("o_bias_s", [P, D])}
        cos_t = sb("cos_t", [P, L])
        sin_t = sb("sin_t", [P, L])
        ident = sb("ident", [P, P])
        ident_b = sb("ident_b", [P, P], BF16)
        causal_kq = sb("causal_kq", [P, P], BF16)
        causal_qk = sb("causal_qk", [P, P], BF16)
        guide = sb("guide", [P, D])
        minus_half = sb("minus_half", [P, T * H])
        reg_big = sb("reg_big", [P, NB * T])

        x_new = sb("x_new", [P, T, D])
        bn = sb("bn", [P, T, 6])
        mean_var = sb("mean_var", [P, T, 2])
        var_eps = sb("var_eps", [P, T])
        rstd = sb("rstd", [P, T])
        xn = sb("xn", [P, T, D])
        xn_t = sb("xn_t", [P, KT, L])
        qk_f = sb("qk_f", [P, 4, L])
        sines = {"k": sb("k_sines", [P, 2, L])}
        rest = {"q": sb("rest_q", [P, 2, L]), "k": sines["k"]}
        parts = sb("parts", [P, 4, 3, L], BF16)
        q_stack = [sb(f"q_stack{i}", [P, H, L], BF16) for i in range(2)]
        k_stack = [sb(f"k_stack{i}", [P, H, L], BF16) for i in range(2)]
        qx = [sb(f"qx{i}", [P, H, XW], BF16) for i in range(2)]
        values = [sb(f"values{i}", [P, T, H, VW]) for i in range(2)]
        neg_max = sb("neg_max", [P, G, T])
        shift_parts = sb("shift_parts", [P, 2, G * T], BF16)
        shift_rows = sb("shift_rows", [2 * G * T, P], BF16)
        probs = [sb(f"probs{i}", [P, G, 2 * L]) for i in range(2)]
        x_neg_max = sb("x_neg_max", [P, 1])
        x_probs_both = sb("x_probs_both", [P, 2, L])
        x_probs = x_probs_both[:, 0, :]
        x_probs_t = x_probs_both[:, 1, :].rearrange("p (t c) -> p t c", t=T)
        sines["q"] = x_probs_both
        out_sums = sb("out_sums", [P, L])
        inv_sum = sb("inv_sum", [P, T * G])
        x_inv = sb("x_inv", [P, G])
        x_half = sb("x_half", [P, G])
        x_out = sb("x_out", [P, G, DH])
        att = [sb(f"att{i}", [P, T, D]) for i in range(2)]
        att_t = sb("att_t", [P, KT, L])
        x_res = sb("x_res", [P, T, D])

        prod = probs[0][:, 0, :].rearrange("p (t d) -> p t d", t=T)
        square = probs[1][:, 0, :].rearrange("p (t d) -> p t d", t=T)
        per_batch = T * H
        dots, inv_norms, norms = (t[:, :, :].rearrange("p t d -> p (t d)") for t in (att[0], att[1], att_t))
        guide_norms = sb("guide_norms", [P, 2, H])
        sim = sb("sim", [P, NB * T])
        extremes = sb("extremes", [P, 2])
        all_extremes = sb("all_extremes", [P, 2])
        spread = sb("spread", [P, 2])
        cls = sb("cls", [P, 3, NB * T])
        class_rows = sb("class_rows", [P, 4, NB * T], BF16)
        class_t = sb("class_t", [P, 2, P], BF16)

        st = [ps(f"scores_t{i}", [P, 2 * L]) for i in range(2)]
        sm = [ps(f"scores{i}", [P, L]) for i in range(2)]
        o_ps = ps("o_ps", [P, L])
        turn_ps = ps("turn_ps", [P, L])
        turn_heads = turn_ps[:, :].rearrange("p (a c) -> p a c", c=VW)
        turn_b = turn_ps[:, 0:P // 2].bitcast(BF16)
        turn_b2 = turn_ps[:, P // 2:P].bitcast(BF16)

        def turn_steps(kind, b):
            return [(off, (k, i)) for slot in range(H) for k, off, i in turns_of(kind, b, slot)]

        turn_args = (turn_steps, lambda kind: PREPARE + [("sh", 0)], finish_turns)
        turn_full = Count(sem("turn_full"), steps_of(*turn_args))
        turn_free = Count(sem("turn_free"), steps_of(*turn_args))

        def max_steps(kind, b):
            res = []
            for slot in range(H):
                m = max_head(b, slot)
                for t in range(T):
                    if t == T - 1 and kind == SPLIT and slot % G == 1:
                        res.append((0, ("extra", slot // G)))
                    if m:
                        res.append((m[0], (m[1], t)))
            return res

        max_args = (max_steps, lambda kind: [(h, t) for h in range(AHEAD) for t in range(T)])
        sm_full = Count(sem("scores_full"), steps_of(*max_args))
        max_done = Count(sem("max_done"), steps_of(*max_args))

        chunks = (lambda kind, b: [(0, lab) for slot in range(H) for lab in chunks_of(slot)],)
        groups = (lambda kind, b: [(0, (g,)) for g in range(NG)],)
        tiles = (lambda kind, b: [(0, (g, kt)) for g in range(NG) for kt in range(T)],)
        st_full = Count(sem("scores_t_full"), steps_of(*chunks))
        exp_done = Count(sem("exp_done"), steps_of(*chunks))
        pv_done = Count(sem("pv_done"), steps_of(*tiles))
        o_taken = Count(sem("o_taken"), steps_of(*groups))
        o_inv = Count(sem("o_inv"), steps_of(*groups))

        def per_group_shift(kind, b):
            return [(off, (i,)) for slot in range(H) for k, off, i in turns_of(kind, b, slot) if k == "sh"]

        shift_args = (per_group_shift, lambda kind: [(0,)])
        shift_high = Count(sem("shift_high"), steps_of(*shift_args))
        shift_ready = Count(sem("shift_ready"), steps_of(*shift_args))
        shift_in = Count(sem("shift_in"), steps_of(*shift_args), 16)

        nexts = (lambda kind, b: [(1, ())] if b + 1 < NB else [], lambda kind: [()])
        x_loaded = Count(sem("x_loaded"), steps_of(*nexts), 16)
        bn_done = Count(sem("bn_done"), steps_of(*nexts))
        stats_done = Count(sem("stats_done"), steps_of(*nexts))
        eps_done = Count(sem("eps_done"), steps_of(*nexts))
        rstd_done = Count(sem("rstd_done"), steps_of(*nexts))
        xn_done = Count(sem("xn_done"), steps_of(*nexts))
        qx_done = Count(sem("qx_done"), steps_of(*nexts))

        def of_next(items):
            return (lambda kind, b: [(1, i) for i in items] if b + 1 < NB else [], lambda kind: list(items))

        stacked = (2 * len(Q_BLOCKS) + 1) * 16
        q_in = Count(sem("q_in"), steps_of(*nexts), stacked)
        k_in = Count(sem("k_in"), steps_of(*nexts), stacked)
        stack_in = {"q": q_in, "k": k_in}
        prep = {side: Count(sem(f"prep_{side}"), steps_of(*of_next([(i,) for i in range(PREP_STEPS)]))) for side in "qk"}

        prevs = (lambda kind, b: [(-1, ())] if b else [], None, lambda kind: [()])
        res_loaded = Count(sem("res_loaded"), steps_of(*prevs), 16)
        res_biased = Count(sem("res_biased"), steps_of(*prevs))
        stored = Count(sem("stored"), steps_of(lambda kind, b: [(-1, ())], None, lambda kind: [()]), 16)

        xmax_exp = Count(sem("extra_exp"), steps_of(lambda kind, b: [(0, (g,)) for g in range(NG)] if kind == SPLIT else []))
        extra_steps = Count(sem("extra_steps"), steps_of(
            lambda kind, b: [(0, (g, i)) for g in range(NG) for i in range(3)] if kind == SPLIT else []))

        consts_in = sem("consts_in")
        preset = sem("preset")
        bias_scaled = sem("bias_scaled")
        masks_cleared = sem("masks_cleared")
        rotary_in = sem("rotary_in")
        c_x = sem("c_x"); c_bn = sem("c_bn"); c_stats = sem("c_stats"); c_eps = sem("c_eps")
        c_rstd = sem("c_rstd"); c_xn = sem("c_xn"); c_tr = sem("c_tr"); c_trc = sem("c_trc")
        c_q = sem("c_q"); c_prod = sem("c_prod"); c_sq = sem("c_sq"); c_dots = sem("c_dots")
        c_norm = sem("c_norm"); c_inv = sem("c_inv"); c_cos = sem("c_cos"); c_simb = sem("c_simb")
        c_sim = sem("c_sim"); c_ext = sem("c_ext"); c_all = sem("c_all"); c_step = sem("c_step")
        c_rows = sem("c_rows"); c_rt = sem("c_rt"); c_rtc = sem("c_rtc"); c_dram = sem("c_dram")
        g_step = sem("g_step")

        still = sem("passed")

        block = ctx.enter_context(nc.Block())

        def run_stage(eng, s, first, body, finish):
            first(Batch(s, 0))
            body(Batch(s, 0))
            with eng.Fori(0, LOOPS, 1) as i:
                body(Batch(s, 1, i))
                body(Batch(s, 2, i))
            body(Batch(s, NB - 1))
            finish(Batch(s, NB - 1))

        def stage_start(eng, s):
            if s:
                eng.wait_ge(stored.sem, 16 * (NB + 1) * s)
            else:
                eng.wait_ge(consts_in, 16 * len(loads))
                eng.wait_ge(preset, PRESETS)

        def prepare(eng, ops, B, side, step, still=None):
            rotary = STAGES[B.s] == ROTARY
            a = 0 if side == "q" else 2
            x, sin_x, low_bits = qk_f[:, a:a + 2, :], sines[side], rest[side]
            high, middle, low = (parts[:, a:a + 2, i, :] for i in range(3))
            both = lambda t: t[:, :].unsqueeze(1).broadcast_to([P, 2, L])
            done = prep[side]
            if step < 4 and not rotary:
                eng.sem_inc(done.sem, 1)
                return
            if step == 3 or (step == 4 and not rotary):
                if B.n:
                    stack_in[side].wait(eng, B + (-1), still=still)
            if step == 0 or (step == 4 and not rotary):
                turn_free.wait(eng, B, "qk", a + 1, still=still)
            else:
                done.wait(eng, B, step - 1, still=still)
            if step == 0:
                last = ops.tensor_tensor(sin_x[:, :, :], x, both(sin_t), ALU.mult)
            elif step == 1:
                last = ops.tensor_tensor(x, x, both(cos_t), ALU.mult)
            elif step == 2:
                ops.tensor_tensor(x[:, 0, :], x[:, 0, :], sin_x[:, 1, :], ALU.subtract)
                last = ops.tensor_tensor(x[:, 1, :], x[:, 1, :], sin_x[:, 0, :], ALU.add)
            elif step == 3:
                last = ops.tensor_copy(high, x)
            elif step == 4:
                last = ops.tensor_tensor(middle, x, high, ALU.subtract)
            elif step == 5:
                last = ops.tensor_tensor(low_bits[:, :, :], x, high, ALU.subtract)
            else:
                last = ops.tensor_tensor(low, low_bits[:, :, :], middle, ALU.subtract)
            last.then_inc(done.sem, 1)

        loads = []
        weights = {k: [(tile[k][:, :, :], w[f"{name}_{k}"].rearrange("(k p) n -> p k n", p=P))
                       for tile, name in ((wq, "wq"), (wk, "wk"), (wv, "wv"), (wo, "wo"))]
                   for k in (CAUSAL, SPLIT, ROTARY)}
        loads += weights[CAUSAL] + weights[SPLIT]
        loads.append((wq_class[:, :, :], w["wq_class"].rearrange("(k p) n -> p k n", p=P)))
        for tile, name in ((qk_bias, "qk_bias"), (v_bias, "v_bias"), (o_bias[CAUSAL], "o_bias_causal"),
                           (o_bias[SPLIT], "o_bias_split"), (guide, "guide")):
            loads.append((tile[:, :], w[name]))
        for tile, name in ((cos_t, "cos"), (sin_t, "sin"), (ident, "ident"), (ident_b, "ident_b"),
                           (causal_kq, "causal_kq"), (causal_qk, "causal_qk"), (reg_big, "reg_big")):
            loads.append((tile[:, :], consts[name]))
        for i in range(2):
            loads.append((qx[i][MASK:MASK + 2, :, :].rearrange("p h c -> p (h c)"), consts["neg_class"]))
        PRESETS = 5 * 2 + 1 + 2
        QX_ROWS = PARTS

        @block.sync
        def _(sp):
            for dst, src in loads:
                sp.dma_start(dst, src).then_inc(consts_in, 16)

            def load_x(B):
                xn_done.wait(sp, B + (-1), still=still)
                sp.dma_start(x_new[:, :, :],
                             xs[B.s][B.one()].rearrange("a (t p) d -> p (a t) d", p=P)).then_inc(x_loaded.sem, 16)

            def load_stack(B, side):
                kind = STAGES[B.s]
                tile, blocks, first_tile, first_mask = ((q_stack, Q_BLOCKS, 0, 0) if side == "q"
                                                        else (k_stack, K_BLOCKS, 2, 2))
                here = stack_in[side].sem
                if B.n >= 2 or B.turn is not None:
                    st_full.wait(sp, B + (-2), H - 1, 1, still=still)
                    if side == "q":
                        qx_done.wait(sp, B + (-2), still=still)
                if B.n:
                    sm_full.wait(sp, B + (-1), 0, 0, still=still)
                if kind == SPLIT:
                    sp.dma_start(tile[B.n % 2][MASK:MASK + 2, :, :],
                                 mask_d[first_mask:first_mask + 2, bass.ds(B.index() * L, L)].unsqueeze(1).broadcast_to([2, H, L])
                                 ).then_inc(here, 16)
                else:
                    sp.sem_inc(here, 16)
                prep[side].wait(sp, B, PREP_STEPS - 1, still=still)
                for j in range(2):
                    for i, part in enumerate(blocks):
                        row = DH * i + 8 * j
                        sp.dma_start(tile[B.n % 2][row:row + 8, :, :], parts[:, first_tile + j, part, :]).then_inc(here, 16)

            def load_residual(B):
                stored.wait(sp, B + (-1), still=still)
                sp.dma_start(x_res[:, :, :],
                             xs[B.s][B.one()].rearrange("a (t p) d -> p (a t) d", p=P)).then_inc(res_loaded.sem, 16)

            def first(B):
                load_x(B)
                load_stack(B, "k")
                load_stack(B, "q")

            def body(B):
                nxt = B.n + 1 < NB
                if nxt:
                    load_x(B + 1)
                if B.n:
                    load_residual(B + (-1))
                if nxt:
                    load_stack(B + 1, "k")
                    load_stack(B + 1, "q")

            def finish(B):
                load_residual(B)

            n_class = 0
            for s, kind in enumerate(STAGES):
                if s:
                    stage_start(sp, s)
                if s == 1:
                    for dst, src in weights[ROTARY]:
                        sp.dma_start(dst, src).then_inc(rotary_in, 16)
                if kind == SPLIT:
                    base = NB * n_class
                    def class_batch(b, base=base):
                        wait_before(sp, c_xn, b, base, still)
                        sp.dma_start(x_new[:, :, :],
                                     xs[s][bass.ds(b, 1)].rearrange("a (t p) d -> p (a t) d", p=P)).then_inc(c_x, 16)

                    over_batches(sp, class_batch)
                    sp.wait_ge(c_rtc, n_class + 1)
                    sp.dma_start(mask_d.rearrange("k (b t) -> (k b) t", t=P).rearrange("(a c) t -> c a t", a=2),
                                 class_t[:, :, :]).then_inc(c_dram, 16)
                    sp.wait_ge(c_dram, 16 * (n_class + 1))
                    n_class += 1
                run_stage(sp, s, first, body, finish)
            sp.wait_ge(stored.sem, 16 * (NB + 1) * len(STAGES))

        @block.gpsimd
        def _(pool):
            for i in range(2):
                nc.gpsimd.memset(values[i][:, :, :, DH:DH + 1], 1.0).then_inc(preset, 1)
                nc.gpsimd.memset(values[i][:, :, :, DH + 1:VW], 0.0).then_inc(preset, 1)
            nc.gpsimd.memset(minus_half[:, :], -0.5).then_inc(preset, 1)
            stage_start(pool, 0)

            def deviation(B):
                stats_done.wait(pool, B, still=still)
                nc.gpsimd.tensor_scalar(var_eps[:, :], mean_var[:, :, 1], EPS, None, ALU.add).then_inc(eps_done.sem, 1)
                eps_done.wait(pool, B, still=still)
                nc.gpsimd.tensor_tensor(rstd[:, :], var_eps[:, :], minus_half[:, 0:T], ALU.pow).then_inc(rstd_done.sem, 1)

            def bias_residual(B):
                res_loaded.wait(pool, B, still=still)
                kind = STAGES[B.s]
                if kind == ROTARY:
                    pool.sem_inc(res_biased.sem, 1)
                else:
                    nc.gpsimd.tensor_tensor(x_res[:, :, :], x_res[:, :, :],
                                            o_bias[kind][:, :].unsqueeze(1).broadcast_to([P, T, D]),
                                            ALU.add).then_inc(res_biased.sem, 1)

            def first(B):
                deviation(B)

            def body(B):
                if B.n + 1 < NB:
                    deviation(B + 1)
                    for step in range(PREP_STEPS):
                        prepare(pool, nc.gpsimd, B + 1, "k", step, still)
                if B.n:
                    bias_residual(B + (-1))

            n_class = 0
            for s, kind in enumerate(STAGES):
                if s:
                    stage_start(pool, s)
                if kind == SPLIT:
                    base = NB * n_class
                    if n_class == 0:
                        pool.wait_ge(g_step, 2)
                        nc.gpsimd.tensor_tensor(guide_norms[:, 0, :], guide_norms[:, 1, :], minus_half[:, 0:H], ALU.pow).then_inc(g_step, 1)
                    def deviation_class(b, base=base):
                        wait_reg(pool, c_stats, b + (base + 1), still)
                        nc.gpsimd.tensor_scalar(var_eps[:, :], mean_var[:, :, 1], EPS, None, ALU.add).then_inc(c_eps, 1)
                        wait_reg(pool, c_eps, b + (base + 1), still)
                        nc.gpsimd.tensor_tensor(rstd[:, :], var_eps[:, :], minus_half[:, 0:T], ALU.pow).then_inc(c_rstd, 1)

                    def inverse_norms(b, base=base):
                        wait_reg(pool, c_norm, b + (base + 1), still)
                        here = bass.ds(b * per_batch, per_batch)
                        nc.gpsimd.tensor_tensor(inv_norms[:, here], norms[:, here], minus_half[:, :], ALU.pow).then_inc(c_inv, 1)

                    one_ahead(pool, deviation_class, inverse_norms)
                    pool.wait_ge(c_ext, n_class + 1)
                    nc.gpsimd.partition_all_reduce(all_extremes[:, :], extremes[:, :], P, bass.bass_isa.ReduceOp.max).then_inc(c_all, 1)
                    n_class += 1
                run_stage(pool, s, first, body, bias_residual)

        @block.vector
        def _(dve):
            for i in range(2):
                nc.vector.memset(q_stack[i][PARTS:ROWS, :, :], 0.0).then_inc(preset, 1)
                nc.vector.memset(k_stack[i][PARTS:ROWS, :, :], 1.0).then_inc(preset, 1)
                nc.vector.memset(qx[i][0:QX_ROWS, :, :], 0.0).then_inc(preset, 1)
            nc.vector.memset(sm[0][:, :], 0.0).then_inc(preset, 1)
            nc.vector.memset(sm[1][:, :], 0.0).then_inc(preset, 1)
            stage_start(dve, 0)

            def statistics(B):
                x_loaded.wait(dve, B)
                for t in range(T):
                    last = nc.vector.bn_stats(bn[:, t, :], x_new[:, t, :])
                last.then_inc(bn_done.sem, 1)
                if B.n:
                    xn_done.wait(dve, B + (-1))
                bn_done.wait(dve, B, still=still)
                for t in range(T):
                    last = nc.vector.bn_aggr(mean_var[:, t, :], bn[:, t, :])
                last.then_inc(stats_done.sem, 1)

            def normalise(B):
                rstd_done.wait(dve, B)
                if B.n:
                    turn_full.wait(dve, B + (-1), "xt", 1)
                for t in range(T):
                    last = nc.vector.tensor_scalar(xn[:, t, :], x_new[:, t, :], mean_var[:, t, 0:1],
                                                   rstd[:, t:t + 1], ALU.subtract, ALU.mult)
                last.then_inc(xn_done.sem, 1)

            def register_queries(B):
                if STAGES[B.s] == SPLIT:
                    q_in.wait(dve, B)
                    if B.n >= 2 or B.turn is not None:
                        sm_full.wait(dve, B + (-2), "extra", NG - 1)
                    nc.vector.tensor_copy(qx[B.n % 2][0:PARTS, :, 0:8],
                                          q_stack[B.n % 2][0:PARTS, :, 0:8]).then_inc(qx_done.sem, 1)
                else:
                    dve.sem_inc(qx_done.sem, 1)

            def maximum(B, h, t):
                kind = STAGES[B.s]
                if h % G == 0 and t == 0 and (h or B.n):
                    shift_ready.wait(dve, B + (0 if h else -1), (h // G - 1) % NG)
                sm_full.wait(dve, B, h, t)
                n = (t + 1) * P if kind == CAUSAL else L
                bank = sm[sm_full.position(B, h, t) % 2]
                nc.vector.tensor_reduce(neg_max[:, h % G, t:t + 1], bank[:, 0:n], AX.X, ALU.max,
                                        negate=True).then_inc(max_done.sem, 1)

            def shift(B, g):
                max_done.wait(dve, B, G * g + G - 1, T - 1)
                if g or B.n:
                    turn_full.wait(dve, B + (0 if g else -1), "sh", (g - 1) % NG)
                nm = neg_max[:, :, :].rearrange("p h t -> p (h t)")
                nc.vector.tensor_copy(shift_parts[:, 0, :], nm).then_inc(shift_high.sem, 1)
                shift_high.wait(dve, B, g)
                nc.vector.tensor_tensor(shift_parts[:, 1, :], nm, shift_parts[:, 0, :],
                                        ALU.subtract).then_inc(shift_ready.sem, 1)

            def extra_max(B, g):
                sm_full.wait(dve, B, "extra", g)
                if g or B.n:
                    xmax_exp.wait(dve, B + (0 if g else -1), (g - 1) % NG)
                bank = sm[sm_full.position(B, "extra", g) % 2]
                nc.vector.tensor_reduce(x_neg_max[:, :], bank[:, :], AX.X, ALU.max, negate=True).then_inc(max_done.sem, 1)

            def scale_output(B, g):
                turn_full.wait(dve, B, "og", g)
                if g or B.n:
                    turn_free.wait(dve, B + (0 if g else -1), "og", (g - 1) % NG)
                nc.vector.reciprocal(inv_sum[:, :], turn_heads[:, :, DH]).then_inc(o_inv.sem, 1)
                if B.n >= 2 or B.turn is not None:
                    turn_full.wait(dve, B + (-2), "ot", 1)
                o_inv.wait(dve, B, g)
                nc.vector.tensor_tensor(
                    att[B.n % 2][:, :, G * DH * g:G * DH * (g + 1)].rearrange("p t (h c) -> p t h c", h=G),
                    turn_heads[:, :, 0:DH].rearrange("p (t h) c -> p t h c", t=T),
                    inv_sum[:, :].rearrange("p (t h) -> p t h", t=T).unsqueeze(3).broadcast_to([P, T, G, DH]),
                    ALU.mult).then_inc(turn_free.sem, 1)

            def mean_of_classes(B, g):
                turn_full.wait(dve, B, "xo", g)
                turn_free.wait(dve, B, "og", g)
                nc.vector.reciprocal(x_inv[0:REG, :], turn_heads[0:REG, 0:G, DH]).then_inc(extra_steps.sem, 1)
                extra_steps.wait(dve, B, g, 0)
                nc.vector.tensor_scalar(x_half[0:REG, :], x_inv[0:REG, :], 0.5, None, ALU.mult).then_inc(extra_steps.sem, 1)
                extra_steps.wait(dve, B, g, 1)
                nc.vector.tensor_tensor(x_out[0:REG, :, :], turn_heads[0:REG, 0:G, 0:DH],
                                        x_half[0:REG, :].unsqueeze(2).broadcast_to([REG, G, DH]), ALU.mult).then_inc(extra_steps.sem, 1)
                extra_steps.wait(dve, B, g, 2)
                reg = att[B.n % 2][0:REG, 0, G * DH * g:G * DH * (g + 1)]
                nc.vector.scalar_tensor_tensor(out=reg, in0=reg, scalar=0.5,
                                               in1=x_out[0:REG, :, :].rearrange("p h c -> p (h c)"),
                                               op0=ALU.mult, op1=ALU.add).then_inc(turn_free.sem, 1)

            def take_turn(B, k, i):
                kind = STAGES[B.s]
                if B.turn is None and B.n < 0:
                    turn_full.wait_earlier(dve, B, 0, k, i)
                    dve.sem_inc(turn_free.sem, 1)
                elif k == "v" and kind == CAUSAL:
                    turn_full.wait(dve, B, k, i)
                    if B.n >= 2 or B.turn is not None:
                        pv_done.wait(dve, B + (-2), NG - 1, T - 1)
                    for t in range(2):
                        last = nc.vector.tensor_tensor(
                            values[B.n % 2][:, 2 * i + t, :, 0:DH],
                            turn_ps[:, D * t:D * (t + 1)].rearrange("p (h c) -> p h c", h=H),
                            v_bias[:, :].rearrange("p (h c) -> p h c", h=H), ALU.add)
                    last.then_inc(turn_free.sem, 1)
                elif k == "sh":
                    turn_full.wait(dve, B, k, i)
                    if i or B.n:
                        shift_in.wait(dve, B + (0 if i else -1), (i - 1) % NG)
                    nc.vector.tensor_copy(shift_rows[:, :], turn_b[0:2 * G * T, :]).then_inc(turn_free.sem, 1)
                elif k == "og":
                    scale_output(B, i)
                elif k == "xo":
                    mean_of_classes(B, i)
                elif k == "out":
                    turn_full.wait(dve, B, k, i)
                    res_biased.wait(dve, B)
                    half = x_res[:, 2 * i:2 * i + 2, :].rearrange("p t d -> p (t d)")
                    nc.vector.tensor_tensor(half, turn_ps[:, :], half, ALU.add).then_inc(turn_free.sem, 1)

            def first(B):
                statistics(B)
                normalise(B)
                for side in "kq":
                    for step in range(PREP_STEPS):
                        prepare(dve, nc.vector, B, side, step)
                if STAGES[B.s] == CAUSAL:
                    take_turn(B, "v", 0)
                    take_turn(B, "v", 1)
                for h in range(AHEAD):
                    for t in range(T):
                        maximum(B, h, t)
                    if h == G - 1:
                        shift(B, 0)
                take_turn(B, "sh", 0)
                register_queries(B)

            def body(B):
                kind = STAGES[B.s]
                if B.n + 1 < NB:
                    statistics(B + 1)

                def prepare_next(slot, place):
                    if B.n + 1 < NB:
                        if (slot, place) == NORMALISE_AT:
                            normalise(B + 1)
                        for step in range(PREP_STEPS):
                            if (slot, place) == PREPARE_AT[step]:
                                prepare(dve, nc.vector, B + 1, "q", step)

                for slot in range(H):
                    m = max_head(B.n, slot)
                    for place in range(2):
                        if m:
                            maximum(B + m[0], m[1], 2 * place)
                        if place and kind == SPLIT and slot % G == 1:
                            extra_max(B, slot // G)
                        if m:
                            maximum(B + m[0], m[1], 2 * place + 1)
                        if place == 0:
                            for k, off, i in turns_of(kind, B.n, slot, 0):
                                take_turn(B + off, k, i)
                            prepare_next(slot, 0)
                    if m and m[1] % G == G - 1:
                        shift(B + m[0], m[1] // G)
                    for k, off, i in turns_of(kind, B.n, slot, 1):
                        take_turn(B + off, k, i)
                    prepare_next(slot, 1)
                if B.n + 1 < NB:
                    register_queries(B + 1)

            def finish(B):
                for k, i in finish_turns(STAGES[B.s]):
                    take_turn(B, k, i)

            n_class = 0

            for s, kind in enumerate(STAGES):
                if s:
                    stage_start(dve, s)
                if kind == ROTARY:
                    for i in range(2):
                        nc.vector.memset(q_stack[i][MASK:MASK + 2, :, :], 0.0).then_inc(masks_cleared, 1)
                if kind == SPLIT:
                    base = NB * n_class
                    if n_class == 0:
                        nc.vector.tensor_tensor(prod[:, 0, :], guide[:, :], guide[:, :], ALU.mult).then_inc(g_step, 1)
                        dve.wait_ge(g_step, 1)
                        nc.vector.tensor_reduce(guide_norms[:, 1, :], prod[:, 0, :].rearrange("p (h c) -> p h c", h=H),
                                                AX.X, ALU.add).then_inc(g_step, 1)
                        dve.wait_ge(g_step, 3)
                        nc.vector.tensor_tensor(guide[:, :].rearrange("p (h c) -> p h c", h=H),
                                                guide[:, :].rearrange("p (h c) -> p h c", h=H),
                                                guide_norms[:, 0, :].unsqueeze(2).broadcast_to([P, H, DH]), ALU.mult).then_inc(g_step, 1)
                        dve.wait_ge(g_step, 4)
                    def class_statistics(b, base=base):
                        dve.wait_ge(c_x, (b + (base + 1)) * 16)
                        for t in range(T):
                            last = nc.vector.bn_stats(bn[:, t, :], x_new[:, t, :])
                        last.then_inc(c_bn, 1)
                        wait_before(dve, c_xn, b, base)
                        wait_reg(dve, c_bn, b + (base + 1), still)
                        for t in range(T):
                            last = nc.vector.bn_aggr(mean_var[:, t, :], bn[:, t, :])
                        last.then_inc(c_stats, 1)

                    def normalised(b, base=base):
                        dve.wait_ge(c_rstd, b + (base + 1))
                        wait_before(dve, c_tr, b, base)
                        for t in range(T):
                            last = nc.vector.tensor_scalar(xn[:, t, :], x_new[:, t, :], mean_var[:, t, 0:1],
                                                           rstd[:, t:t + 1], ALU.subtract, ALU.mult)
                        last.then_inc(c_xn, 1)

                    def similarity(b, base=base):
                        dve.wait_ge(c_q, b + (base + 1))
                        wait_before(dve, c_dots, b, base)
                        here = bass.ds(b * per_batch, per_batch)
                        for t in range(T):
                            last = nc.vector.tensor_tensor(prod[:, t, :], st[0][:, D * t:D * (t + 1)], guide[:, :], ALU.mult)
                        last.then_inc(c_prod, 1)
                        dve.wait_ge(c_prod, b + (base + 1))
                        nc.vector.tensor_reduce(dots[:, here], prod.rearrange("p t (h c) -> p (t h) c", h=H),
                                                AX.X, ALU.add).then_inc(c_dots, 1)
                        dve.wait_ge(c_sq, b + (base + 1))
                        nc.vector.tensor_reduce(norms[:, here], square.rearrange("p t (h c) -> p (t h) c", h=H),
                                                AX.X, ALU.add).then_inc(c_norm, 1)

                    one_ahead(dve, class_statistics, similarity, normalised)
                    dve.wait_ge(c_dots, NB * (n_class + 1))
                    dve.wait_ge(c_inv, NB * (n_class + 1))
                    nc.vector.tensor_tensor(dots, dots, inv_norms, ALU.mult).then_inc(c_cos, 1)
                    dve.wait_ge(c_cos, n_class + 1)
                    nc.vector.tensor_reduce(sim[:, :], dots.rearrange("p (t h) -> p t h", h=H),
                                            AX.X, ALU.add).then_inc(c_simb, 1)
                    dve.wait_ge(c_simb, n_class + 1)
                    nc.vector.tensor_scalar(sim[:, :], sim[:, :], 1.0 / H, None, ALU.mult).then_inc(c_sim, 1)
                    steps = [0]

                    def link(ins):
                        steps[0] += 1
                        ins.then_inc(c_step, 1)
                        dve.wait_ge(c_step, STEPS * n_class + steps[0])

                    STEPS = 15
                    dve.wait_ge(c_sim, n_class + 1)
                    link(nc.vector.tensor_tensor(cls[:, 0, :], sim[:, :], reg_big[:, :], ALU.add))
                    link(nc.vector.tensor_reduce(spread[:, 0:1], cls[:, 0, :], AX.X, ALU.min))
                    link(nc.vector.tensor_tensor(cls[:, 1, :], sim[:, :], reg_big[:, :], ALU.subtract))
                    link(nc.vector.tensor_scalar(extremes[:, 0:1], spread[:, 0:1], -1.0, None, ALU.mult))
                    nc.vector.tensor_reduce(extremes[:, 1:2], cls[:, 1, :], AX.X, ALU.max).then_inc(c_ext, 1)
                    dve.wait_ge(c_all, n_class + 1)
                    link(nc.vector.tensor_tensor(spread[:, 0:1], all_extremes[:, 1:2], all_extremes[:, 0:1], ALU.add))
                    link(nc.vector.reciprocal(spread[:, 1:2], spread[:, 0:1]))
                    link(nc.vector.tensor_scalar(cls[:, 0, :], sim[:, :], all_extremes[:, 0:1], spread[:, 1:2],
                                                 ALU.add, ALU.mult))
                    link(nc.vector.tensor_scalar(cls[:, 1, :], cls[:, 0, :], 0.9, None, ALU.is_gt))
                    link(nc.vector.tensor_scalar(cls[:, 2, :], reg_big[:, :], 0.0, None, ALU.is_gt))
                    link(nc.vector.tensor_tensor(cls[:, 0, :], cls[:, 1, :], cls[:, 2, :], ALU.max))
                    link(nc.vector.tensor_copy(class_rows[:, 0, :], cls[:, 0, :]))
                    link(nc.vector.tensor_scalar(class_rows[:, 1, :], cls[:, 0, :], -1.0, 1.0, ALU.mult, ALU.add))
                    link(nc.vector.tensor_scalar(class_rows[:, 2, :], cls[:, 0, :], BIG, -BIG, ALU.mult, ALU.add))
                    link(nc.vector.tensor_tensor(cls[:, 0, :], cls[:, 0, :], cls[:, 2, :], ALU.subtract))
                    link(nc.vector.tensor_scalar(class_rows[:, 3, :], cls[:, 0, :], -BIG, None, ALU.mult))
                    assert steps[0] == STEPS
                    dve.sem_inc(c_rows, 1)
                    dve.wait_ge(c_rt, n_class + 1)
                    nc.vector.tensor_copy(class_t[:, 0, :], turn_b)
                    nc.vector.tensor_copy(class_t[:, 1, :], turn_b2).then_inc(c_rtc, 1)
                    n_class += 1
                run_stage(dve, s, first, body, finish)

        @block.scalar
        def _(act):
            stage_start(act, 0)
            nc.scalar.mul(q_bias[:, :], qk_bias[:, 0:KT], DH ** -0.5).then_inc(bias_scaled, 1)

            def exponential(B, h, c, i):
                kind = STAGES[B.s]
                st_full.wait(act, B, h, c)
                g = h // G
                if h % G == 0 and (g or B.n):
                    pv_done.wait(act, B + (0 if g else -1), (g - 1) % NG, 2 * c + 1)
                n = chunk_offset(kind, 2 * c + 1) + L - key_start(kind, 2 * c + 1)
                nc.scalar.activation(probs[c][:, h % G, 0:n], st[i][:, 0:n], ACT.Exp).then_inc(exp_done.sem, 1)

            def take_sums(B, g):
                pv_done.wait(act, B, g, T - 1)
                if g or B.n:
                    turn_full.wait(act, B + (0 if g else -1), "og", (g - 1) % NG)
                nc.scalar.copy(out_sums[:, :], o_ps[:, :]).then_inc(o_taken.sem, 1)

            def extra_exp(B, g):
                max_done.wait(act, B, "extra", g)
                if g or B.n:
                    turn_full.wait(act, B + (0 if g else -1), "ex", (g - 1) % NG)
                bank = sm[sm_full.position(B, "extra", g) % 2]
                nc.scalar.activation(x_probs, bank[:, :], ACT.Exp, bias=x_neg_max[:, :]).then_inc(xmax_exp.sem, 1)

            def shift_dma(B, g):
                turn_free.wait(act, B, "sh", g)
                act.dma_start(q_stack[B.n % 2][SHIFT:SHIFT + 2, G * g:G * g + G, :],
                              shift_rows[:, :]).then_inc(shift_in.sem, 16)

            def take_turn(B, k, i):
                kind = STAGES[B.s]
                if B.turn is None and B.n < 0:
                    return
                if k == "xt":
                    turn_full.wait(act, B, k, i)
                    nc.scalar.copy(xn_t[:, i, :], turn_ps[:, :]).then_inc(turn_free.sem, 1)
                elif k == "qk":
                    turn_full.wait(act, B, k, i)
                    side = "q" if i < 2 else "k"
                    if B.n:
                        prep[side].wait(act, B + (-1), PREP_STEPS - 1)
                        if kind != ROTARY:
                            stack_in[side].wait(act, B + (-1))
                    scale = DH ** -0.5 if i < 2 else 1.0
                    if kind == CAUSAL:
                        bias = q_bias[:, i:i + 1] if i < 2 else qk_bias[:, i:i + 1]
                        project = lambda dst: nc.scalar.activation(dst, turn_ps[:, :], ACT.Identity, bias=bias, scale=scale)
                    else:
                        project = lambda dst: nc.scalar.activation(dst, turn_ps[:, :], ACT.Copy, scale=scale)
                    last = project(qk_f[:, i, :])
                    if kind != ROTARY:
                        last = project(parts[:, i, 0, :])
                    last.then_inc(turn_free.sem, 1)
                elif k == "v" and kind != CAUSAL:
                    turn_full.wait(act, B, k, i)
                    if B.n >= 2 or B.turn is not None:
                        pv_done.wait(act, B + (-2), NG - 1, T - 1)
                    for t in range(2):
                        last = nc.scalar.copy(values[B.n % 2][:, 2 * i + t, :, 0:DH],
                                              turn_ps[:, D * t:D * (t + 1)].rearrange("p (h c) -> p h c", h=H))
                    last.then_inc(turn_free.sem, 1)
                elif k == "ot":
                    turn_full.wait(act, B, k, i)
                    nc.scalar.copy(att_t[:, i, :], turn_ps[:, :]).then_inc(turn_free.sem, 1)
                elif k == "ex":
                    turn_full.wait(act, B, k, i)
                    if i or B.n:
                        turn_full.wait(act, B + (0 if i else -1), "xo", (i - 1) % NG)
                    nc.scalar.copy(x_probs_both[:, 1, :], turn_ps[:, :]).then_inc(turn_free.sem, 1)

            def store(B):
                turn_free.wait(act, B, "out", 1)
                act.dma_start(xs[B.s + 1][B.one()].rearrange("a (t p) d -> p (a t) d", p=P),
                              x_res[:, :, :]).then_inc(stored.sem, 16)

            def first(B):
                if B.s == 0:
                    act.wait_ge(bias_scaled, 1)
                for k, i in PREPARE:
                    take_turn(B, k, i)
                shift_dma(B, 0)

            def body(B):
                kind = STAGES[B.s]
                for slot in range(H):
                    off, g, kt = values_of(slot)
                    for place, (h, c) in enumerate(chunks_of(slot)):
                        exponential(B, h, c, place)
                        if place and kind == SPLIT and slot % G == 1:
                            extra_exp(B, slot // G)
                        if place and kt == T - 1 and B.n + off >= 0:
                            take_sums(B + off, g)
                        for k, o, i in turns_of(kind, B.n, slot, place):
                            take_turn(B + o, k, i)
                        if place and slot == STORE_AT:
                            if B.n:
                                store(B + (-1))
                            else:
                                act.sem_inc(stored.sem, 16)
                        if not place:
                            for k, o, i in turns_of(kind, B.n, slot - 1, 1):
                                if k == "sh":
                                    shift_dma(B + o, i)

            def finish(B):
                take_sums(B, NG - 1)
                for k, i in finish_turns(STAGES[B.s]):
                    take_turn(B, k, i)
                store(B)

            n_class = 0
            for s, kind in enumerate(STAGES):
                if s:
                    stage_start(act, s)
                if kind == SPLIT:
                    base = NB * n_class
                    def class_batch(b, base=base):
                        act.wait_ge(c_tr, b + (base + 1))
                        nc.scalar.copy(xn_t[:, :, :].rearrange("p k t -> p (k t)"), st[1][:, :]).then_inc(c_trc, 1)
                        act.wait_ge(c_prod, b + (base + 1))
                        wait_before(act, c_norm, b, base)
                        nc.scalar.activation(square.rearrange("p t d -> p (t d)"), st[0][:, :], ACT.Square).then_inc(c_sq, 1)

                    over_batches(act, class_batch)
                    n_class += 1
                run_stage(act, s, first, body, finish)

        @block.tensor
        def _(pe):
            stage_start(pe, 0)

            def score_rows(kind, shifted):
                return ROWS if shifted else (SHIFT if kind == SPLIT else PARTS)

            def max_tiles(B, h, tiles, slot_in_group):
                kind = STAGES[B.s]
                if h == 0 and 0 in tiles:
                    q_in.wait(pe, B)
                    k_in.wait(pe, B)
                r = score_rows(kind, False)
                q, k = q_stack[B.n % 2], k_stack[B.n % 2]
                for t in tiles:
                    max_done.wait_earlier(pe, B, 2, h, t)
                    if t == 0 and slot_in_group is not None:
                        xmax_exp.wait(pe, *slot_in_group)
                    n = (t + 1) * P if kind == CAUSAL else L
                    bank = sm[sm_full.position(B, h, t) % 2]
                    last = nc.tensor.matmul(bank[:, 0:n], q[0:r, h, t * P:(t + 1) * P], k[0:r, h, 0:n],
                                            start=True, stop=kind != CAUSAL)
                    if kind == CAUSAL:
                        last = nc.tensor.matmul(bank[:, t * P:(t + 1) * P], ident_b[:, :], causal_qk[:, :],
                                                start=False, stop=True)
                    last.then_inc(sm_full.sem, 1)

            def extra_tile(B, g):
                qx_done.wait(pe, B)
                max_done.wait_earlier(pe, B, 2, "extra", g)
                bank = sm[sm_full.position(B, "extra", g) % 2]
                for i in range(G):
                    h = G * g + i
                    last = nc.tensor.matmul(bank[XW * i:XW * (i + 1), :], qx[B.n % 2][0:SHIFT, h, :],
                                            k_stack[B.n % 2][0:SHIFT, h, :], start=True, stop=True)
                last.then_inc(sm_full.sem, 1)

            def scores_t(B, h, c, i):
                kind = STAGES[B.s]
                if h % G == 0 and c == 0:
                    shift_in.wait(pe, B, h // G)
                if kind == ROTARY and B.n == 0 and h == 0:
                    pe.wait_ge(masks_cleared, 2)
                q, k = q_stack[B.n % 2], k_stack[B.n % 2]
                exp_done.wait_earlier(pe, B, 2, h, c)
                for kt in (2 * c, 2 * c + 1):
                    q0 = key_start(kind, kt)
                    off = chunk_offset(kind, kt)
                    last = nc.tensor.matmul(st[i][:, off:off + L - q0], k[0:ROWS, h, kt * P:(kt + 1) * P],
                                            q[0:ROWS, h, q0:L], start=True, stop=kind != CAUSAL)
                    if kind == CAUSAL:
                        last = nc.tensor.matmul(st[i][:, off:off + P], ident_b[:, :], causal_kq[:, :],
                                                start=False, stop=True)
                last.then_inc(st_full.sem, 1)

            def output_sums(B, g, kt, half):
                kind = STAGES[B.s]
                if half == 0:
                    exp_done.wait(pe, B, G * g + G - 1, kt // 2)
                if g == 0 and kt == 0 and half == 0:
                    turn_free.wait(pe, B, "v", 1)
                if kt == 0 and half == 0 and (g or B.n):
                    o_taken.wait(pe, B + (0 if g else -1), (g - 1) % NG)
                q0, off = key_start(kind, kt), chunk_offset(kind, kt)
                for h in (2 * half, 2 * half + 1):
                    last = nc.tensor.matmul(o_ps[VW * h:VW * (h + 1), q0:L], values[B.n % 2][:, kt, G * g + h, :],
                                            probs[kt // 2][:, h, off:off + L - q0], start=kt == 0, stop=kt == T - 1)
                if half:
                    last.then_inc(pv_done.sem, 1)

            def turn(B, k, i):
                kind = STAGES[B.s]
                if B.turn is None and B.n < 0:
                    turn_free.wait_earlier(pe, B, 1, k, i)
                    pe.sem_inc(turn_full.sem, 1)
                    return
                if k == "xt":
                    xn_done.wait(pe, B)
                elif k == "sh":
                    shift_ready.wait(pe, B, i)
                elif k == "ex":
                    xmax_exp.wait(pe, B, i)
                elif k == "og":
                    o_taken.wait(pe, B, i)
                turn_free.wait_earlier(pe, B, 1, k, i)
                if k == "xt":
                    for t in range(T):
                        last = nc.tensor.transpose(turn_ps[:, t * P:(t + 1) * P], xn[:, t, i * P:(i + 1) * P], ident[:, :])
                elif k == "qk":
                    weight = (wq if i < 2 else wk)[kind]
                    m = i % 2
                    for kt in range(KT):
                        last = nc.tensor.matmul(turn_ps[:, :], weight[:, kt, m * P:(m + 1) * P], xn_t[:, kt, :],
                                                start=kt == 0, stop=kt == KT - 1)
                elif k == "v":
                    for j in range(2):
                        t = 2 * i + j
                        for kt in range(KT):
                            last = nc.tensor.matmul(turn_ps[:, j * D:(j + 1) * D], xn_t[:, kt, t * P:(t + 1) * P],
                                                    wv[kind][:, kt, :], start=kt == 0, stop=kt == KT - 1)
                elif k == "sh":
                    last = nc.tensor.transpose(turn_b[0:2 * G * T, :],
                                               shift_parts[:, :, :].rearrange("p a c -> p (a c)"), ident_b[:, :])
                elif k == "ex":
                    for t in range(T):
                        last = nc.tensor.transpose(turn_ps[:, t * P:(t + 1) * P], x_probs_both[:, 0, t * P:(t + 1) * P], ident[:, :])
                elif k == "og":
                    for t in range(T):
                        last = nc.tensor.transpose(turn_ps[:, t * P:(t + 1) * P], out_sums[:, t * P:(t + 1) * P], ident[:, :])
                elif k == "xo":
                    for h in range(G):
                        for kt in range(T):
                            last = nc.tensor.matmul(turn_heads[0:8, h, :], x_probs_t[:, kt, XW * h:XW * h + 8],
                                                    values[B.n % 2][:, kt, G * i + h, :], start=kt == 0, stop=kt == T - 1)
                elif k == "ot":
                    for t in range(T):
                        last = nc.tensor.transpose(turn_ps[:, t * P:(t + 1) * P], att[B.n % 2][:, t, i * P:(i + 1) * P], ident[:, :])
                elif k == "out":
                    for j in range(2):
                        t = 2 * i + j
                        for kt in range(KT):
                            last = nc.tensor.matmul(turn_ps[:, j * D:(j + 1) * D], att_t[:, kt, t * P:(t + 1) * P],
                                                    wo[kind][:, kt, :], start=kt == 0, stop=kt == KT - 1)
                last.then_inc(turn_full.sem, 1)

            def first(B):
                for k, i in PREPARE:
                    turn(B, k, i)
                for h in range(AHEAD):
                    max_tiles(B, h, range(T), None)
                turn(B, "sh", 0)

            def body(B):
                kind = STAGES[B.s]
                for slot in range(H):
                    m = max_head(B.n, slot)
                    after_extra = (B, slot // G) if kind == SPLIT and slot % G == 2 else None

                    def max_tile(t):
                        if m:
                            max_tiles(B + m[0], m[1], [t], after_extra)

                    def turns(place):
                        for k, off, i in turns_of(kind, B.n, slot, place):
                            turn(B + off, k, i)

                    (h0, c), (h1, _) = chunks_of(slot)
                    off, g, kt = values_of(slot)
                    scores_t(B, h0, c, 0)
                    max_tile(0)
                    max_tile(1)
                    turns(0)
                    scores_t(B, h1, c, 1)
                    max_tile(2)
                    if kind == SPLIT and slot % G == 1:
                        extra_tile(B, slot // G)
                    if B.n + off >= 0:
                        output_sums(B + off, g, kt, 0)
                    max_tile(3)
                    if B.n + off >= 0:
                        output_sums(B + off, g, kt, 1)
                    turns(1)

            def finish(B):
                for kt in (T - 2, T - 1):
                    for half in range(2):
                        output_sums(B, NG - 1, kt, half)
                for k, i in finish_turns(STAGES[B.s]):
                    turn(B, k, i)

            n_class = 0
            for s, kind in enumerate(STAGES):
                if s:
                    stage_start(pe, s)
                if kind == ROTARY:
                    pe.wait_ge(rotary_in, 16 * len(weights[ROTARY]))
                if kind == SPLIT:
                    base = NB * n_class
                    def class_batch(b, base=base):
                        pe.wait_ge(c_xn, b + (base + 1))
                        wait_before(pe, c_trc, b, base)
                        for kt in range(KT):
                            for t in range(T):
                                last = nc.tensor.transpose(st[1][:, kt * L + t * P:kt * L + (t + 1) * P],
                                                           xn[:, t, kt * P:(kt + 1) * P], ident[:, :])
                        last.then_inc(c_tr, 1)
                        pe.wait_ge(c_trc, b + (base + 1))
                        wait_before(pe, c_prod, b, base)
                        wait_before(pe, c_sq, b, base)
                        for t in range(T):
                            for kt in range(KT):
                                last = nc.tensor.matmul(st[0][:, D * t:D * (t + 1)], xn_t[:, kt, t * P:(t + 1) * P],
                                                        wq_class[:, kt, :], start=kt == 0, stop=kt == KT - 1)
                        last.then_inc(c_q, 1)

                    over_batches(pe, class_batch)
                    pe.wait_ge(c_rows, n_class + 1)
                    rows = class_rows[:, :, :].rearrange("p k c -> p (k c)")
                    nc.tensor.transpose(turn_b, rows[:, 0:P], ident_b[:, :])
                    nc.tensor.transpose(turn_b2, rows[:, P:2 * P], ident_b[:, :]).then_inc(c_rt, 1)
                    n_class += 1
                run_stage(pe, s, first, body, finish)


def kernel(**inputs):
    import ml_dtypes
    import numpy as np
    import concourse.bacc as bacc
    from concourse.bass_utils import run_bass_kernel_spmd

    a = {k: np.asarray(v) for k, v in inputs.items()}

    def by_feature(m):
        return m.reshape(D, H, DH).transpose(0, 2, 1).reshape(D, D)

    def columns(v):
        return v.reshape(H, DH).transpose(1, 0).reshape(KT, P).transpose(1, 0)

    def on_all(v):
        return np.broadcast_to(v.reshape(1, D), (P, D))

    w = {}
    for kind, q, k, v, o in (
        (CAUSAL, a["L0_attn_a_Wq"].T, a["L0_attn_a_Wk"].T, a["L0_attn_a_Wv"].T, a["L0_attn_a_Wo"].T),
        (SPLIT, *np.split(a["L0_ffn_W_qkv"], 3, axis=1), a["L0_ffn_W_proj"]),
        (ROTARY, *np.split(a["L0_attn_b_Wqkv"], 3, axis=1), a["L0_attn_b_Wo"]),
    ):
        w[f"wq_{kind}"], w[f"wk_{kind}"], w[f"wv_{kind}"], w[f"wo_{kind}"] = by_feature(q), by_feature(k), v, o
        if kind == SPLIT:
            w["wq_class"] = q
    w["qk_bias"] = np.concatenate([columns(a["L0_attn_a_bq"]), columns(a["L0_attn_a_bk"])], axis=1)
    w["v_bias"] = on_all(a["L0_attn_a_bv"])
    w["o_bias_causal"] = on_all(a["L0_attn_a_bo"])
    w["o_bias_split"] = on_all(a["L0_ffn_b_proj"])
    w["guide"] = on_all(a["L0_ffn_g_info"][0, 0])

    freq = (1.0 / np.float32(10000.0) ** (np.arange(0, DH, 2, dtype=np.float32) / np.float32(DH))).astype(np.float32)
    angle = np.outer(freq, np.arange(L, dtype=np.float32)).astype(np.float32)
    later = np.arange(P)[:, None] > np.arange(P)[None, :]
    c = {
        "cos": np.repeat(np.cos(angle), H, axis=0).astype(np.float32),
        "sin": np.repeat(np.sin(angle), H, axis=0).astype(np.float32),
        "ident": np.eye(P, dtype=np.float32),
        "ident_b": np.eye(P).astype(ml_dtypes.bfloat16),
        "causal_kq": np.where(later, -BIG, 0.0).astype(ml_dtypes.bfloat16),
        "causal_qk": np.where(later.T, -BIG, 0.0).astype(ml_dtypes.bfloat16),
        "reg_big": np.where((np.arange(P)[:, None] < REG) & (np.arange(NB * T)[None, :] % T == 0), 1e30, 0.0).astype(np.float32),
        "neg_class": np.repeat(np.array([[0.0], [1.0]]), H * XW, axis=1).astype(ml_dtypes.bfloat16),
    }

    nc = bacc.Bacc("TRN2", target_bir_lowering=False, num_devices=1)
    arrays = {}

    def put(name, value):
        value = np.ascontiguousarray(value)
        arrays[name] = value
        return nc.dram_tensor(name, value.shape, mybir.dt.from_np(value.dtype), kind="ExternalInput").ap()

    x_in = put("x", a["L0_attn_a_x"])
    w = {n: put("w_" + n, v) for n, v in w.items()}
    c = {n: put("c_" + n, v) for n, v in c.items()}
    out = nc.dram_tensor("out", (NB, L, D), F32, kind="ExternalOutput").ap()
    hybrid_blocks(nc, x_in, w, c, out)
    result = run_bass_kernel_spmd(nc, [arrays], core_ids=[0])
    return result.results[0]["out"]
```
